# Optimizing a Trainium2 kernel written in Bass

```python
import numpy as np
import jax
import jax.numpy as jnp

def _softmax(x, axis=-1):
    return jax.nn.softmax(x, axis=axis)

def _gelu(x):
    return jax.nn.gelu(x, approximate=True)

def _silu(x):
    return jax.nn.silu(x)

def _sigmoid(x):
    return jax.nn.sigmoid(x)

def _layernorm(x, axis=-1, eps=1e-05):
    m = jnp.mean(x, axis=axis, keepdims=True)
    v = jnp.var(x, axis=axis, keepdims=True)
    return (x - m) / jnp.sqrt(v + eps)

def _scatter_add(tgt, idx, src, axis=0):
    return tgt.at[idx].add(src)

def _segment_sum(src, seg, n):
    return jax.ops.segment_sum(src, seg, n)
kernel_name = 'mk_adj_resnorm_d1_adj_r2_9131c3'

def setup_inputs(seed: int=0):
    np.random.seed(seed)
    _w = jnp.asarray

    def _rec_inputs():
        import jax
        import jax.numpy as jnp
        _gk = jax.random.key(seed)
        x = -0.0005963 + 1.001 * jax.random.normal(jax.random.fold_in(_gk, 1), (2048, 256), jnp.float32)
        _a = jax.random.bernoulli(jax.random.fold_in(_gk, 2), 0.00390625, (2048, 2048))
        _af = _a.astype(jnp.float32)
        adj = _af
        return (x, adj)
    x, adj = _rec_inputs()

    def _L0_gnn_setup():
        import jax, jax.numpy as jnp
        import numpy as np
        N = 3072
        D_IN = 256
        D_OUT = 256
        DENSITY = 0.005
        key = jax.random.key(seed)
        ks = jax.random.split(key, 12)
        x = jax.random.normal(ks[0], (N, D_IN), dtype=jnp.float32)
        adj_a = (jax.random.uniform(ks[1], (N, N)) < DENSITY).astype(jnp.float32)
        adj_b = (jax.random.uniform(ks[2], (N, N)) < DENSITY).astype(jnp.float32)
        W_sa = jax.random.normal(ks[3], (D_IN, D_OUT), dtype=jnp.float32) * (1.414 / np.sqrt(D_IN + D_OUT))
        a_sa = jax.random.normal(ks[4], (1, 2 * D_OUT), dtype=jnp.float32) * (1.414 / np.sqrt(1 + 2 * D_OUT))
        stdv = 1.0 / np.sqrt(D_OUT)
        W_gcnb = jax.random.uniform(ks[5], (D_IN, D_OUT), minval=-stdv, maxval=stdv, dtype=jnp.float32)
        b_gcnb = jax.random.uniform(ks[6], (D_OUT,), minval=-stdv, maxval=stdv, dtype=jnp.float32)
        s = 1.0 / np.sqrt(2 * D_IN)
        Wa = jax.random.uniform(ks[7], (1, 2 * D_IN), minval=-s, maxval=s, dtype=jnp.float32)
        ba = jax.random.uniform(ks[8], (1,), minval=-s, maxval=s, dtype=jnp.float32)
        Wb = jax.random.uniform(ks[9], (1, 2 * D_IN), minval=-s, maxval=s, dtype=jnp.float32)
        bb = jax.random.uniform(ks[10], (1,), minval=-s, maxval=s, dtype=jnp.float32)
        return {'x': x, 'adj_a': adj_a, 'adj_b': adj_b, 'W_sa': W_sa, 'a_sa': a_sa, 'W_gcnb': W_gcnb, 'b_gcnb': b_gcnb, 'Wa': Wa, 'ba': ba, 'Wb': Wb, 'bb': bb}
    _L0_gnn_all = _L0_gnn_setup()
    _L0_gnn_in = {k: v for k, v in _L0_gnn_all.items() if k in ('W_sa', 'a_sa', 'W_gcnb', 'b_gcnb', 'Wa', 'ba', 'Wb', 'bb')}
    del _L0_gnn_all
    return {'x': x, 'adj': adj, 'L0_gnn_W_sa': _L0_gnn_in['W_sa'], 'L0_gnn_a_sa': _L0_gnn_in['a_sa'], 'L0_gnn_W_gcnb': _L0_gnn_in['W_gcnb'], 'L0_gnn_b_gcnb': _L0_gnn_in['b_gcnb'], 'L0_gnn_Wa': _L0_gnn_in['Wa'], 'L0_gnn_ba': _L0_gnn_in['ba'], 'L0_gnn_Wb': _L0_gnn_in['Wb'], 'L0_gnn_bb': _L0_gnn_in['bb']}

def reference(x, adj, L0_gnn_W_sa, L0_gnn_a_sa, L0_gnn_W_gcnb, L0_gnn_b_gcnb, L0_gnn_Wa, L0_gnn_ba, L0_gnn_Wb, L0_gnn_bb):
    import jax
    import jax.numpy as jnp

    def _L0_gnn_ref(x, adj_a, adj_b, W_sa, a_sa, W_gcnb, b_gcnb, Wa, ba, Wb, bb):
        import jax, jax.numpy as jnp
        import numpy as np
        N = 3072
        D_IN = 256
        D_OUT = 256
        DENSITY = 0.005
        type_sum_a = adj_a @ x
        type_sum_b = adj_b @ x
        attn_a = jax.nn.sigmoid(jnp.concatenate([type_sum_a, x], axis=1) @ Wa.T + ba)
        attn_b = jax.nn.sigmoid(jnp.concatenate([type_sum_b, x], axis=1) @ Wb.T + bb)
        h = x @ W_sa
        Hd = h.shape[1]
        s_left = h @ a_sa[0, :Hd]
        s_right = h @ a_sa[0, Hd:]
        scores = s_left[:, None] + s_right[None, :]
        e = jnp.where(adj_a != 0, jnp.exp(-jax.nn.leaky_relu(scores, 0.01)), 0.0)
        attn = e / (jnp.sum(e, axis=1, keepdims=True) + 1e-05)
        x_a = attn @ h
        x_b = adj_b @ (x @ W_gcnb) + b_gcnb
        return jax.nn.sigmoid(attn_a * x_a + attn_b * x_b)
    x = _layernorm(x + _L0_gnn_ref(x, adj, adj, L0_gnn_W_sa, L0_gnn_a_sa, L0_gnn_W_gcnb, L0_gnn_b_gcnb, L0_gnn_Wa, L0_gnn_ba, L0_gnn_Wb, L0_gnn_bb), axis=-1)
    return x

_drawn_inputs = setup_inputs


def setup_inputs(seed=0):
    import zlib

    import numpy as np

    out = dict(_drawn_inputs(seed))
    spreads = {}
    factors = {'L0_gnn_a_sa': 2.762, 'L0_gnn_b_gcnb': 8.0, 'L0_gnn_Wa': 2.769}
    for name, (base, spread) in spreads.items():
        noise = np.random.default_rng([zlib.crc32(name.encode()), seed]).standard_normal(out[name].shape)
        drawn = base * np.exp(spread * noise) if base else spread * noise
        out[name] = jnp.asarray(drawn.astype(out[name].dtype))
    for name, factor in factors.items():
        out[name] = (out[name] * factor).astype(out[name].dtype)
    return out
```

```python
from contextlib import ExitStack

import concourse.bass as bass
from concourse import mybir

P = 128
F32 = mybir.dt.float32
BF16 = mybir.dt.bfloat16
FP16 = mybir.dt.float16
I32 = mybir.dt.int32
ALU = mybir.AluOpType
ACT = mybir.ActivationFunctionType
AX_X = mybir.AxisListType.X

SLOPE = 0.01
DEN_EPS = 1e-5
LN_EPS = 1e-5
EXP_ROOM = 80.0
ROW_SIZE = 4096.0
EXPONENT = 0x7F800000

CHUNK_BLOCKS = 2
GROUP = 4


def build(nc, x, adj, w_sa, a_sa, w_gcnb, b_gcnb, wa, ba, wb, bb, out):
    n, d = x.shape
    T = n // P
    KH = d // P
    CI = CHUNK_BLOCKS * P
    CHUNKS = n // CI
    GROUPS = T // GROUP
    HC = d + 4
    GC = d + 2
    MC = d + 2
    LOOP_PAIRS = (CHUNKS - 2) // 2
    MATS = 3

    x_v = x.rearrange("(t p) d -> p t d", p=P)
    adj_v = adj.rearrange("(q p) m -> q p m", p=P)
    out_v = out.rearrange("(q p) d -> q p d", p=P)

    with ExitStack() as ctx:
        def sb(name, shape, dt):
            return ctx.enter_context(nc.sbuf_tensor(name, shape, dt))

        def sem(name):
            return ctx.enter_context(nc.semaphore(name))

        x_sb = sb("x_sb", [P, T, d], F32)
        adj_raw = sb("adj_raw", [P, 2, CHUNK_BLOCKS, n], F32)
        left = sb("left", [P, 2, MATS, T, CI], BF16)
        right = sb("right", [P, MATS, T, 2, MC], FP16)
        s_left_row = sb("s_left_row", [P, n], F32)
        hx = sb("hx", [P, T, HC], F32)
        gx = sb("gx", [P, T, GC], F32)
        w_all = sb("w_all", [P, KH, HC + GC], F32)
        b_bc = sb("b_bc", [P, d], F32)
        gate_b = sb("gate_b", [P, 2], F32)
        xT = sb("xT", [P, 2, d], F32)
        ident_f = sb("ident_f", [P, P], F32)
        ident_b = sb("ident_b", [P, P], BF16)
        ones = sb("ones", [P, P], F32)
        diag = sb("diag", [P, GROUP, P], F32)
        row_max = sb("row_max", [P, T, 2], F32)
        row_top = sb("row_top", [P, T], F32)
        row_pow = sb("row_pow", [P, T], F32)
        row_inv = sb("row_inv", [P, T], F32)
        s_clip = sb("s_clip", [P, 2, T], F32)
        s_neg = sb("s_neg", [P, T], F32)
        u_raw = sb("u_raw", [P, 2, T], F32)
        p_raw = sb("p_raw", [P, 2, T], F32)
        p_top = sb("p_top", [P, 2, T], BF16)
        p_gate = sb("p_gate", [P, 2, T], F32)
        p_rec = sb("p_rec", [P, 2, T], F32)
        p_rest = sb("p_rest", [P, 2, T], F32)
        scale = sb("scale", [P, MATS, T], F32)
        uv = sb("uv", [P, T, 2], F32)
        gate_x = sb("gate_x", [P, T, 2], F32)
        z = sb("z", [P, 2, 2], F32)
        attn = sb("attn", [P, 2, 2], F32)
        den_b = sb("den_b", [P, 2, 1], F32)
        den = sb("den", [P, 2, 1], F32)
        rden = sb("rden", [P, 2, 1], F32)
        alpha = sb("alpha", [P, 2, 2], F32)
        xb = sb("xb", [P, 2, d], F32)
        mix = sb("mix", [P, 2, d], F32)
        y = sb("y", [P, 2, d], F32)
        stats = sb("stats", [P, 2, 6], F32)
        mean_var = sb("mean_var", [P, 2, 2], F32)
        var_eps = sb("var_eps", [P, 2, 1], F32)
        minus_half = sb("minus_half", [P, 1], F32)
        rstd = sb("rstd", [P, 2, 1], F32)
        y_out = sb("y_out", [P, 2, d], F32)

        a_bc = y[:, :, :].rearrange("p b d -> p (b d)")
        a_prod = mix[:, 0, :]

        tp_bank = [ctx.enter_context(nc.psum_tensor(f"tp_bank{i}", [P, 512], F32)) for i in range(2)]
        acc = [ctx.enter_context(nc.psum_tensor(f"acc{i}", [P, 512], F32)) for i in range(2 * MATS)]
        h_bank, g_bank, s_bank = acc[0:2], acc[2:4], acc[4:6]

        w_loaded = sem("w_loaded")
        small_loaded = sem("small_loaded")
        x_loaded = [sem(f"x_loaded{g}") for g in range(GROUPS)]
        adj_loaded = [sem(f"adj_loaded{i}") for i in range(2)]
        consts_zeroed = sem("consts_zeroed")
        consts_ready = sem("consts_ready")
        w_vecs_ready = sem("w_vecs_ready")
        xT_in_psum = sem("xT_in_psum")
        xT_ready = sem("xT_ready")
        hg_in_psum = sem("hg_in_psum")
        hg_copied = sem("hg_copied")
        row_max_ready = sem("row_max_ready")
        cols = sem("cols")
        exps_ready = sem("exps_ready")
        scale_ready = sem("scale_ready")
        high_ready = sem("high_ready")
        low_ready = sem("low_ready")
        diag_ready = sem("diag_ready")
        s_row_in_psum = sem("s_row_in_psum")
        s_row_ready = sem("s_row_ready")
        adjT_in_psum = sem("adjT_in_psum")
        a_ready = sem("a_ready")
        gates_ready = sem("gates_ready")
        bc_ready = sem("bc_ready")
        sums_ready = sem("sums_ready")
        sums_read = sem("sums_read")
        z_ready = sem("z_ready")
        attn_ready = sem("attn_ready")
        den_b_ready = sem("den_b_ready")
        den_ready = sem("den_ready")
        rden_ready = sem("rden_ready")
        alpha_ready = sem("alpha_ready")
        xb_gated_ready = sem("xb_gated_ready")
        mix_b_ready = sem("mix_b_ready")
        sig_ready = sem("sig_ready")
        y_ready = sem("y_ready")
        stats_ready = sem("stats_ready")
        mean_var_ready = sem("mean_var_ready")
        var_eps_ready = sem("var_eps_ready")
        rstd_ready = sem("rstd_ready")
        out_ready = sem("out_ready")
        out_stored = [sem(f"out_stored{b}") for b in range(2)]

        def adj_bf16(par, b, t):
            words = adj_raw[:, par, b, :].bitcast(BF16).rearrange("p (m two) -> p m two", two=2)
            return words[:, t * P:(t + 1) * P, 1]

        def is_first(c):
            return isinstance(c, int) and c == 0

        def tp_slot(g, u):
            bank = tp_bank[g % 2][:, :].bitcast(BF16)
            return bank[:, u * CI:(u + 1) * CI]

        block = ctx.enter_context(nc.Block())

        @block.sync
        def _(sp):
            def load_adj(c, par):
                for b in range(CHUNK_BLOCKS):
                    sp.dma_start(adj_raw[:, par, b, :], adj_v[bass.ds(c * CHUNK_BLOCKS + b, 1), :, :]
                                 .rearrange("q p m -> p (q m)")).then_inc(adj_loaded[par], 16)

            def store_chunk(c):
                for b in range(CHUNK_BLOCKS):
                    sp.wait_ge(out_ready, c * CHUNK_BLOCKS + b + 1)
                    sp.dma_start(out_v[bass.ds(c * CHUNK_BLOCKS + b, 1), :, :].rearrange("q p d -> p (q d)"),
                                 y_out[:, b, :]).then_inc(out_stored[b], 16)

            def step(c, par, load):
                if load:
                    sp.wait_ge(adjT_in_psum, (c + 2) * GROUPS)
                    load_adj(c + 3, 1 - par)
                store_chunk(c)

            for g in range(GROUPS):
                sp.dma_start(x_sb[:, g * GROUP:(g + 1) * GROUP, :],
                             x_v[:, g * GROUP:(g + 1) * GROUP, :]).then_inc(x_loaded[g], 16)
            load_adj(0, 0)
            load_adj(1, 1)
            sp.wait_ge(adjT_in_psum, GROUPS)
            load_adj(2, 0)
            with sp.Fori(0, (CHUNKS - 4) // 2) as k:
                for par in range(2):
                    step(2 * k + par, par, True)
            for c in range(CHUNKS - 4, CHUNKS):
                step(c, c % 2, c + 3 < CHUNKS)
            for b in range(CHUNK_BLOCKS):
                sp.wait_ge(out_stored[b], 16 * CHUNKS)

        @block.tensor
        def _(pe):
            pe.wait_ge(consts_ready, 3)

            def transpose_x(t):
                if t % GROUP == 0:
                    pe.wait_ge(x_loaded[t // GROUP], 16)
                if t >= 2:
                    pe.wait_ge(xT_ready, t - 1)
                for k in range(KH):
                    mm = nc.tensor.transpose(tp_bank[t % 2][:, k * P:(k + 1) * P],
                                             x_sb[:, t, k * P:(k + 1) * P], ident_f[:, :])
                mm.then_inc(xT_in_psum, 1)

            def project(t):
                pe.wait_ge(xT_ready, t + 1)
                if t >= 2:
                    pe.wait_ge(hg_copied, t - 1)
                for bank, c0, c1 in ((h_bank, 0, HC), (g_bank, HC, HC + GC)):
                    for k in range(KH):
                        mm = nc.tensor.matmul(bank[t % 2][:, 0:c1 - c0], xT[:, t % 2, k * P:(k + 1) * P],
                                              w_all[:, k, c0:c1], start=(k == 0), stop=(k == KH - 1))
                mm.then_inc(hg_in_psum, 1)

            transpose_x(0)
            pe.wait_ge(w_loaded, 16 * 6)
            pe.wait_ge(w_vecs_ready, 2 * KH)
            for t in range(T):
                if t + 1 < T:
                    transpose_x(t + 1)
                project(t)

            def transpose_group(c, par, rnd, g, first=False):
                if g == 0:
                    pe.wait_ge(adj_loaded[par], 16 * CHUNK_BLOCKS * rnd)
                if first and g < 2:
                    pe.wait_ge(xT_ready, T)
                else:
                    pe.wait_ge(a_ready, c * GROUPS + g - 1)
                for u in range(GROUP):
                    for b in range(CHUNK_BLOCKS):
                        mm = nc.tensor.transpose(tp_slot(g, u)[:, b * P:(b + 1) * P],
                                                 adj_bf16(par, b, g * GROUP + u), ident_b[:, :])
                mm.then_inc(adjT_in_psum, 1)

            for g in range(GROUPS):
                transpose_group(0, 0, 1, g, first=True)

            for g in range(GROUPS):
                pe.wait_ge(diag_ready, GROUP * (g + 1))
                if g >= 2:
                    pe.wait_ge(s_row_ready, g - 1)
                nc.tensor.matmul(s_bank[g % 2][:, :], ones[:, :], diag[:, :, :].rearrange("p a b -> p (a b)"),
                                 start=True, stop=True).then_inc(s_row_in_psum, 1)

            def product(c, par, b, m, first):
                for t in range(T):
                    g = t // GROUP
                    if b == 0 and t % GROUP == 0:
                        if m == 0:
                            pe.wait_ge(a_ready, c * GROUPS + g + 1)
                        else:
                            pe.wait_ge(bc_ready, 2 * (c * GROUPS + g) + m)
                    if first:
                        pe.wait_ge(high_ready, m * T + t + 1)
                        pe.wait_ge(low_ready, m * T + t + 1)
                    for half in range(2):
                        mm = nc.tensor.matmul(acc[b * MATS + m][:, 0:MC],
                                              left[:, par, m, t, b * P:(b + 1) * P],
                                              right[:, m, t, half, :],
                                              start=(t == 0 and half == 0), stop=(t == T - 1 and half == 1))
                return mm

            def step(k, par, nxt, first=False):
                c = 2 * k + par
                for b in range(CHUNK_BLOCKS):
                    q = c * CHUNK_BLOCKS + b
                    for m in range(MATS):
                        if b == 0 and nxt:
                            transpose_group(c + 1, 1 - par, k + par + 1, m)
                            if m == MATS - 1:
                                transpose_group(c + 1, 1 - par, k + par + 1, GROUPS - 1)
                        if m == 0:
                            if first:
                                pe.wait_ge(hg_copied, T)
                                pe.wait_ge(s_row_ready, GROUPS)
                            else:
                                pe.wait_ge(sums_read, q - 1)
                        mm = product(c, par, b, m, first and b == 0)
                    mm.then_inc(sums_ready, 1)

            step(0, 0, True, first=True)
            step(0, 1, True)
            with pe.Fori(1, LOOP_PAIRS) as k:
                for par in range(2):
                    step(k, par, True)
            step(LOOP_PAIRS, 0, True)
            step(LOOP_PAIRS, 1, False)

        @block.scalar
        def _(act):
            act.dma_start(w_all[:, :, 0:d], w_sa.rearrange("(k p) n -> p k n", p=P)).then_inc(w_loaded, 16)
            act.dma_start(w_all[:, :, HC:HC + d], w_gcnb.rearrange("(k p) n -> p k n", p=P)).then_inc(w_loaded, 16)
            act.dma_start(a_bc, a_sa[0, :].partition_broadcast(P)).then_inc(small_loaded, 16)
            for row, c1, c2 in ((wa, HC + d, d + 2), (wb, HC + d + 1, d + 3)):
                for half, col in ((0, c1), (1, c2)):
                    act.dma_start(w_all[:, :, col:col + 1],
                                  row[0:1, half * d:(half + 1) * d].rearrange("a (k p) -> p k a", p=P),
                                  allow_slow_non_contiguous=True).then_inc(w_loaded, 16)
            act.dma_start(b_bc[:, :], b_gcnb.partition_broadcast(P)).then_inc(small_loaded, 16)
            act.dma_start(gate_b[:, 0:1], ba.partition_broadcast(P)).then_inc(small_loaded, 16)
            act.dma_start(gate_b[:, 1:2], bb.partition_broadcast(P)).then_inc(small_loaded, 16)

            def copy_xT(t):
                act.wait_ge(xT_in_psum, t + 1)
                if t >= 2:
                    act.wait_ge(hg_in_psum, t - 1)
                nc.scalar.activation(xT[:, t % 2, :], tp_bank[t % 2][:, 0:d], ACT.Copy).then_inc(xT_ready, 1)

            def copy_hg(t):
                act.wait_ge(hg_in_psum, t + 1)
                nc.scalar.activation(hx[:, t, :], h_bank[t % 2][:, 0:HC], ACT.Copy)
                nc.scalar.activation(gx[:, t, :], g_bank[t % 2][:, 0:GC], ACT.Copy).then_inc(hg_copied, 1)

            copy_xT(0)
            for t in range(T):
                if t + 1 < T:
                    copy_xT(t + 1)
                copy_hg(t)

            act.wait_ge(cols, 1)
            nc.scalar.activation(u_raw[:, 0, :], s_clip[:, 0, :], ACT.Exp, scale=-1.0)
            nc.scalar.activation(u_raw[:, 1, :], hx[:, :, d], ACT.Exp, scale=-SLOPE)
            nc.scalar.activation(p_raw[:, 0, :], hx[:, :, d + 1], ACT.Exp, scale=-SLOPE)
            nc.scalar.activation(p_raw[:, 1, :], s_clip[:, 1, :], ACT.Exp, scale=-1.0).then_inc(exps_ready, 1)

            def copy_a(c, par, g, recycled=True):
                if g == 0 and recycled:
                    act.wait_ge(sums_ready, (c - 1) * CHUNK_BLOCKS)
                act.wait_ge(adjT_in_psum, c * GROUPS + g + 1)
                for u in range(GROUP):
                    t = g * GROUP + u
                    op = nc.scalar.activation(left[:, par, 0, t, :], tp_slot(g, u), ACT.Copy,
                                              scale=row_pow[:, t:t + 1])
                op.then_inc(a_ready, 1)

            def high(m, t):
                src = gx[:, t, :] if m == 0 else hx[:, t, 0:d]
                dst = right[:, m, t, 0, 0:GC if m == 0 else d]
                nc.scalar.activation(dst, src, ACT.Copy, scale=scale[:, m, t:t + 1]).then_inc(high_ready, 1)

            act.wait_ge(scale_ready, 1)
            for t in range(T):
                high(0, t)
                if t % GROUP == GROUP - 1:
                    copy_a(0, 0, t // GROUP, recycled=False)
            for g in range(GROUPS):
                act.wait_ge(s_row_in_psum, g + 1)
                nc.scalar.activation(s_left_row[:, g * 512:(g + 1) * 512], s_bank[g % 2][:, :],
                                     ACT.Copy).then_inc(s_row_ready, 1)
            act.wait_ge(scale_ready, 2)
            for m in (1, 2):
                for t in range(T):
                    high(m, t)

            def epilogue(c, b):
                q = c * CHUNK_BLOCKS + b
                act.wait_ge(z_ready, q + 1)
                nc.scalar.activation(attn[:, b, :], z[:, b, :], ACT.Sigmoid).then_inc(attn_ready, 1)
                act.wait_ge(attn_ready, q + 1)
                nc.scalar.activation(xb[:, b, :], xb[:, b, :], ACT.Copy,
                                     scale=attn[:, b, 1:2]).then_inc(xb_gated_ready, 1)
                act.wait_ge(sums_read, q + 1)
                nc.scalar.activation(mix[:, b, :], mix[:, b, :], ACT.Sigmoid).then_inc(sig_ready, 1)

            def step(c, par, nxt, recycled=True):
                if nxt:
                    for g in range(GROUPS):
                        copy_a(c + 1, 1 - par, g, recycled)
                for b in range(CHUNK_BLOCKS):
                    epilogue(c, b)

            step(0, 0, True, recycled=False)
            step(1, 1, True)
            with act.Fori(1, LOOP_PAIRS) as k:
                for par in range(2):
                    step(2 * k + par, par, True)
            step(CHUNKS - 2, 0, True)
            step(CHUNKS - 1, 1, False)

        @block.vector
        def _(dve):
            dve.wait_ge(small_loaded, 16 * 4)
            dve.wait_ge(w_loaded, 16 * 6)
            done = 0
            for k in range(KH):
                for side in range(2):
                    if done:
                        dve.wait_ge(w_vecs_ready, done)
                    nc.vector.tensor_tensor_reduce(out=a_prod, in0=w_all[:, k, 0:d],
                                                   in1=a_bc[:, side * d:(side + 1) * d], scale=1.0, scalar=0.0,
                                                   op0=ALU.mult, op1=ALU.add,
                                                   accum_out=w_all[:, k, d + side:d + side + 1]
                                                   ).then_inc(w_vecs_ready, 1)
                    done += 1

            for t in range(T):
                dve.wait_ge(hg_copied, t + 1)
                nc.vector.tensor_reduce(row_max[:, t, 0:1], hx[:, t, 0:d], AX_X, ALU.max,
                                        apply_absolute_value=True)
                nc.vector.tensor_reduce(row_max[:, t, 1:2], gx[:, t, :], AX_X, ALU.max,
                                        apply_absolute_value=True).then_inc(row_max_ready, 1)

            nc.vector.tensor_scalar(s_clip[:, :, :], hx[:, :, d:d + 2].rearrange("p t s -> p s t"),
                                    -EXP_ROOM, EXP_ROOM, ALU.max, ALU.min).then_inc(cols, 1)
            dve.wait_ge(row_max_ready, T)
            nc.vector.scalar_tensor_tensor(out=row_top[:, :], in0=row_max[:, :, 0], scalar=1.0,
                                           in1=row_max[:, :, 1], op0=ALU.max, op1=ALU.max).then_inc(cols, 1)
            nc.vector.tensor_scalar(s_neg[:, :], hx[:, :, d + 1], -1.0, None, ALU.mult)
            dve.wait_ge(cols, 2)
            nc.vector.tensor_scalar(row_pow[:, :].bitcast(I32), row_top[:, :].bitcast(I32), EXPONENT, None,
                                    ALU.bitwise_and).then_inc(cols, 1)
            dve.wait_ge(cols, 3)
            nc.vector.tensor_scalar(row_inv[:, :].bitcast(I32), row_pow[:, :].bitcast(I32), EXPONENT, None,
                                    ALU.bitwise_xor).then_inc(cols, 1)
            dve.wait_ge(cols, 4)
            nc.vector.tensor_scalar(scale[:, 0, :], row_inv[:, :], ROW_SIZE / 2, None,
                                    ALU.mult).then_inc(scale_ready, 1)
            dve.wait_ge(exps_ready, 1)
            nc.vector.tensor_copy(p_top[:, :, :], p_raw[:, :, :]).then_inc(cols, 1)
            dve.wait_ge(cols, 5)
            nc.vector.tensor_copy(p_gate[:, :, :], p_top[:, :, :]).then_inc(cols, 1)
            dve.wait_ge(cols, 6)
            nc.vector.reciprocal(p_rec[:, :, :], p_gate[:, :, :]).then_inc(cols, 1)
            dve.wait_ge(cols, 7)
            nc.vector.tensor_tensor(p_rest[:, :, :], p_raw[:, :, :], p_rec[:, :, :], ALU.mult).then_inc(cols, 1)
            dve.wait_ge(cols, 8)
            dve.wait_ge(scale_ready, 1)
            for m in (1, 2):
                op = nc.vector.tensor_tensor(scale[:, m, :], p_rest[:, m - 1, :], scale[:, 0, :], ALU.mult)
            op.then_inc(scale_ready, 1)
            nc.vector.tensor_scalar(uv[:, :, :], u_raw[:, :, :].rearrange("p s t -> p t s"), 1.0 / ROW_SIZE, None,
                                    ALU.mult)
            for s in range(2):
                nc.vector.tensor_scalar(gate_x[:, :, s:s + 1], hx[:, :, d + 2 + s:d + 3 + s], gate_b[:, s:s + 1],
                                        None, ALU.add)
            dve.wait_ge(scale_ready, 2)
            for m in (1, 2):
                op = nc.vector.tensor_copy(right[:, m, :, 0, d], scale[:, m, :])
            op.then_inc(cols, 1)
            nc.vector.memset(right[:, 1:3, :, :, d + 1:d + 2], 0.0)
            dve.wait_ge(cols, 9)
            for m in (1, 2):
                nc.vector.tensor_tensor(right[:, m, :, 1, d], scale[:, m, :], right[:, m, :, 0, d], ALU.subtract)

            for g in range(GROUPS):
                if g >= 1:
                    dve.wait_ge(s_row_in_psum, g)
                for u in range(GROUP):
                    t = g * GROUP + u
                    nc.vector.tensor_scalar(diag[:, u, :], ident_f[:, :], hx[:, t, d:d + 1], None,
                                            ALU.mult).then_inc(diag_ready, 1)

            def low(m, t):
                src = gx[:, t, :] if m == 0 else hx[:, t, 0:d]
                width = GC if m == 0 else d
                dve.wait_ge(high_ready, m * T + t + 1)
                nc.vector.scalar_tensor_tensor(out=right[:, m, t, 1, 0:width], in0=src,
                                               scalar=scale[:, m, t:t + 1], in1=right[:, m, t, 0, 0:width],
                                               op0=ALU.mult, op1=ALU.subtract).then_inc(low_ready, 1)

            def gate_group(c, par, g, recycled=True):
                if g == 0 and recycled:
                    dve.wait_ge(sums_ready, (c - 1) * CHUNK_BLOCKS)
                n_group = c * GROUPS + g
                s_row = s_left_row[:, bass.ds(c * CI, CI)]
                for m, cmp in ((1, ALU.is_lt), (2, ALU.is_ge)):
                    for u in range(GROUP):
                        t = g * GROUP + u
                        op = nc.vector.tensor_scalar(left[:, par, m, t, :], s_row, s_neg[:, t:t + 1],
                                                     p_gate[:, m - 1, t:t + 1], cmp, ALU.mult)
                    op.then_inc(gates_ready, 1)
                dve.wait_ge(a_ready, n_group + 1)
                for m in (1, 2):
                    dve.wait_ge(gates_ready, 2 * n_group + m)
                    grp = left[:, par, m, g * GROUP:(g + 1) * GROUP, :].rearrange("p t i -> p (t i)")
                    a_grp = left[:, par, 0, g * GROUP:(g + 1) * GROUP, :].rearrange("p t i -> p (t i)")
                    nc.vector.tensor_tensor(grp, grp, a_grp, ALU.mult).then_inc(bc_ready, 1)

            def epilogue(c, b):
                q = c * CHUNK_BLOCKS + b
                acc_a, acc_b, acc_c = acc[b * MATS:(b + 1) * MATS]
                dve.wait_ge(sums_ready, q + 1)
                uv_q = uv[:, bass.ds(q, 1), :].rearrange("p q s -> p (q s)")
                gate_q = gate_x[:, bass.ds(q, 1), :].rearrange("p q s -> p (q s)")
                nc.vector.scalar_tensor_tensor(out=z[:, b, :], in0=acc_a[:, d:d + 2], scalar=1.0 / ROW_SIZE,
                                               in1=gate_q, op0=ALU.mult, op1=ALU.add)
                nc.vector.tensor_tensor(den_b[:, b, :], acc_b[:, d:d + 1], uv_q[:, 1:2],
                                        ALU.mult).then_inc(den_b_ready, 1)
                nc.vector.scalar_tensor_tensor(out=xb[:, b, :], in0=acc_a[:, 0:d], scalar=1.0 / ROW_SIZE,
                                               in1=b_bc[:, :], op0=ALU.mult, op1=ALU.add).then_inc(z_ready, 1)
                dve.wait_ge(den_b_ready, q + 1)
                nc.vector.scalar_tensor_tensor(out=den[:, b, :], in0=acc_c[:, d:d + 1], scalar=uv_q[:, 0:1],
                                               in1=den_b[:, b, :], op0=ALU.mult, op1=ALU.add).then_inc(den_ready, 1)
                dve.wait_ge(den_ready, 2 * q + 1)
                nc.vector.tensor_scalar(den[:, b, :], den[:, b, :], DEN_EPS, None, ALU.add).then_inc(den_ready, 1)
                dve.wait_ge(den_ready, 2 * q + 2)
                nc.vector.reciprocal(rden[:, b, :], den[:, b, :]).then_inc(rden_ready, 1)
                dve.wait_ge(rden_ready, q + 1)
                dve.wait_ge(attn_ready, q + 1)
                nc.vector.tensor_scalar(alpha[:, b, :], uv_q, rden[:, b, :], attn[:, b, 0:1], ALU.mult,
                                        ALU.mult).then_inc(alpha_ready, 1)
                dve.wait_ge(alpha_ready, q + 1)
                dve.wait_ge(xb_gated_ready, q + 1)
                nc.vector.scalar_tensor_tensor(out=mix[:, b, :], in0=acc_b[:, 0:d], scalar=alpha[:, b, 1:2],
                                               in1=xb[:, b, :], op0=ALU.mult,
                                               op1=ALU.add).then_inc(mix_b_ready, 1)
                dve.wait_ge(mix_b_ready, q + 1)
                nc.vector.scalar_tensor_tensor(out=mix[:, b, :], in0=acc_c[:, 0:d], scalar=alpha[:, b, 0:1],
                                               in1=mix[:, b, :], op0=ALU.mult, op1=ALU.add).then_inc(sums_read, 1)
                dve.wait_ge(y_ready, q + 1)
                nc.vector.bn_stats(stats[:, b, :], y[:, b, :]).then_inc(stats_ready, 1)
                if b > 0 or not is_first(c):
                    normalise(c, b - 1) if b > 0 else normalise(c - 1, CHUNK_BLOCKS - 1)
                else:
                    dve.wait_ge(stats_ready, q + 1)
                nc.vector.bn_aggr(mean_var[:, b, :], stats[:, b, :]).then_inc(mean_var_ready, 1)
                dve.wait_ge(mean_var_ready, q + 1)
                nc.vector.tensor_scalar(var_eps[:, b, :], mean_var[:, b, 1:2], LN_EPS, None,
                                        ALU.add).then_inc(var_eps_ready, 1)

            def normalise(c, b, more=True):
                q = c * CHUNK_BLOCKS + b
                if more:
                    dve.wait_ge(stats_ready, q + 2)
                dve.wait_ge(rstd_ready, q + 1)
                if not is_first(c):
                    dve.wait_ge(out_stored[b], 16 * c)
                nc.vector.tensor_scalar(y_out[:, b, :], y[:, b, :], mean_var[:, b, 0:1], rstd[:, b, :],
                                        ALU.subtract, ALU.mult).then_inc(out_ready, 1)

            def step(c, par, nxt, recycled=True):
                if nxt:
                    for g in range(GROUPS):
                        gate_group(c + 1, 1 - par, g, recycled)
                for b in range(CHUNK_BLOCKS):
                    epilogue(c, b)

            for t in range(T):
                low(0, t)
            dve.wait_ge(s_row_ready, GROUPS)
            for g in range(GROUPS):
                gate_group(0, 0, g, recycled=False)
            for m in (1, 2):
                for t in range(T):
                    low(m, t)
            step(0, 0, True, recycled=False)
            step(1, 1, True)
            with dve.Fori(1, LOOP_PAIRS) as k:
                for par in range(2):
                    step(2 * k + par, par, True)
            step(CHUNKS - 2, 0, True)
            step(CHUNKS - 1, 1, False)
            normalise(CHUNKS - 1, CHUNK_BLOCKS - 1, more=False)

        @block.gpsimd
        def _(pool):
            nc.gpsimd.memset(ident_f[:, :], 0.0).then_inc(consts_zeroed, 1)
            nc.gpsimd.memset(ident_b[:, :], 0.0).then_inc(consts_zeroed, 1)
            nc.gpsimd.memset(minus_half[:, :], -0.5)
            nc.gpsimd.memset(ones[:, :], 1.0).then_inc(consts_ready, 1)
            pool.wait_ge(consts_zeroed, 2)
            for m in (ident_f, ident_b):
                nc.gpsimd.affine_select(out=m[:, :], in_=m[:, :], compare_op=ALU.not_equal, fill=1.0, base=0,
                                        pattern=[[-1, P]], channel_multiplier=1).then_inc(consts_ready, 1)

            def finish(c, b, recycled):
                q = c * CHUNK_BLOCKS + b
                pool.wait_ge(sig_ready, q + 1)
                if recycled:
                    pool.wait_ge(out_ready, q - 1)
                nc.gpsimd.tensor_tensor(y[:, b, :], x_sb[:, bass.ds(q, 1), :].rearrange("p q d -> p (q d)"),
                                        mix[:, b, :], ALU.add).then_inc(y_ready, 1)
                pool.wait_ge(var_eps_ready, q + 1)
                nc.gpsimd.tensor_tensor(rstd[:, b, :], var_eps[:, b, :], minus_half[:, :],
                                        ALU.pow).then_inc(rstd_ready, 1)

            for b in range(CHUNK_BLOCKS):
                finish(0, b, False)
            with pool.Fori(1, CHUNKS) as c:
                for b in range(CHUNK_BLOCKS):
                    finish(c, b, True)


_INS = ["x", "adj", "L0_gnn_W_sa", "L0_gnn_a_sa", "L0_gnn_W_gcnb", "L0_gnn_b_gcnb",
        "L0_gnn_Wa", "L0_gnn_ba", "L0_gnn_Wb", "L0_gnn_bb"]


def kernel(**inputs):
    import numpy as _np
    import concourse.bacc as _bacc
    from concourse import mybir as _mybir
    from concourse.bass_utils import run_bass_kernel_spmd as _run

    nc = _bacc.Bacc("TRN2", target_bir_lowering=False, num_devices=1)
    arrays, args = {}, []
    for name in _INS:
        a = _np.ascontiguousarray(inputs[name])
        arrays[f"in_{name}_dram"] = a
        args.append(nc.dram_tensor(f"in_{name}_dram", a.shape, _mybir.dt.from_np(a.dtype), kind="ExternalInput").ap())
    o = nc.dram_tensor("out_dram", tuple(inputs["x"].shape), _mybir.dt.float32, kind="ExternalOutput").ap()
    build(nc, *args, o)
    r = _run(nc, [arrays], core_ids=[0])
    return r.results[0]["out_dram"]
```

```python
from contextlib import ExitStack

import concourse.bass as bass
from concourse import mybir

P = 128
F32 = mybir.dt.float32
BF16 = mybir.dt.bfloat16
FP16 = mybir.dt.float16
I32 = mybir.dt.int32
ALU = mybir.AluOpType
ACT = mybir.ActivationFunctionType
AX_X = mybir.AxisListType.X

SLOPE = 0.01
DEN_EPS = 1e-5
LN_EPS = 1e-5
EXP_ROOM = 80.0
ROW_SIZE = 8192.0
EXPONENT = 0x7F800000

CHUNK_BLOCKS = 2
GROUP = 4


def build(nc, x, adj, w_sa, a_sa, w_gcnb, b_gcnb, wa, ba, wb, bb, out):
    n, d = x.shape
    T = n // P
    KH = d // P
    CI = CHUNK_BLOCKS * P
    CHUNKS = n // CI
    GROUPS = T // GROUP
    RC = d + 4
    MC = d + 2
    FROM_G, FROM_H = 0, 1
    S_LEFT, S_RIGHT = d + 2, d + 3
    LOOP_PAIRS = (CHUNKS - 2) // 2
    MATS = 3

    x_v = x.rearrange("(t p) d -> p t d", p=P)
    adj_v = adj.rearrange("(q p) m -> q p m", p=P)
    out_v = out.rearrange("(q p) d -> q p d", p=P)

    with ExitStack() as ctx:
        def sb(name, shape, dt):
            return ctx.enter_context(nc.sbuf_tensor(name, shape, dt))

        def sem(name):
            return ctx.enter_context(nc.semaphore(name))

        x_sb = sb("x_sb", [P, T, d], F32)
        adj_raw = sb("adj_raw", [P, 2, CHUNK_BLOCKS, n], F32)
        left = sb("left", [P, 2, MATS, T, CI], BF16)
        right = sb("right", [P, MATS, T, 2, MC], FP16)
        s_left_row = sb("s_left_row", [P, n], F32)
        proj = sb("proj", [P, T, 2, RC], F32)
        w_all = sb("w_all", [P, 2, KH, RC], F32)
        b_bc = sb("b_bc", [P, d], F32)
        gate_b = sb("gate_b", [P, 2], F32)
        xT = sb("xT", [P, 2, d], F32)
        ident_f = sb("ident_f", [P, P], F32)
        ident_b = sb("ident_b", [P, P], BF16)
        ones = sb("ones", [P, P], F32)
        w_left = sb("w_left", [P, KH, P], F32)
        w_max = sb("w_max", [P, 2], F32)
        x_max = sb("x_max", [P, T], F32)
        row_bound = sb("row_bound", [P, T], F32)
        row_top = sb("row_top", [P, T], F32)
        row_pow = sb("row_pow", [P, T], F32)
        row_inv = sb("row_inv", [P, T], F32)
        left_c = sb("left_c", [P, T], F32)
        s_clip = sb("s_clip", [P, T, 2], F32)
        s_neg = sb("s_neg", [P, T], F32)
        u_raw = sb("u_raw", [P, 2, T], F32)
        q_raw = sb("q_raw", [P, T], F32)
        p_raw = sb("p_raw", [P, T], F32)
        p_top = sb("p_top", [P, T], BF16)
        p_rec = sb("p_rec", [P, T], F32)
        p_rest = sb("p_rest", [P, T], F32)
        scale = sb("scale", [P, MATS, T], F32)
        uv = sb("uv", [P, T, 2], F32)
        gate_x = sb("gate_x", [P, T, 2], F32)
        z = sb("z", [P, 2, 2], F32)
        attn = sb("attn", [P, 2, 2], F32)
        den_b = sb("den_b", [P, 2, 1], F32)
        den = sb("den", [P, 2, 1], F32)
        rden = sb("rden", [P, 2, 1], F32)
        alpha = sb("alpha", [P, 2, 2], F32)
        xb = sb("xb", [P, 2, d], F32)
        mix = sb("mix", [P, 2, d], F32)
        y = sb("y", [P, 2, d], F32)
        stats = sb("stats", [P, 2, 6], F32)
        mean_var = sb("mean_var", [P, 2, 2], F32)
        var_eps = sb("var_eps", [P, 2, 1], F32)
        minus_half = sb("minus_half", [P, 1], F32)
        rstd = sb("rstd", [P, 2, 1], F32)
        y_out = sb("y_out", [P, 2, d], F32)

        a_bc = y[:, :, :].rearrange("p b d -> p (b d)")
        a_prod = mix[:, 0, :]

        tp_bank = [ctx.enter_context(nc.psum_tensor(f"tp_bank{i}", [P, 512], F32)) for i in range(2)]
        sums = ctx.enter_context(nc.psum_tensor("sums", [P, 2 * MATS, 512], F32))
        acc = [sums[:, i, :] for i in range(2 * MATS)]
        proj_bank = [acc[1], acc[2]]
        adj0_bank, s_bank = acc[4], acc[5]

        w_loaded = sem("w_loaded")
        w_sa_loaded = sem("w_sa_loaded")
        a_loaded = sem("a_loaded")
        small_loaded = sem("small_loaded")
        x_loaded = [sem(f"x_loaded{g}") for g in range(GROUPS)]
        adj_loaded = [sem(f"adj_loaded{i}") for i in range(2)]
        consts_zeroed = sem("consts_zeroed")
        consts_ready = sem("consts_ready")
        w_left_ready = sem("w_left_ready")
        w_max_part = sem("w_max_part")
        w_max_ready = sem("w_max_ready")
        pad_ready = sem("pad_ready")
        w_vecs_ready = sem("w_vecs_ready")
        xT_in_psum = sem("xT_in_psum")
        xT_ready = sem("xT_ready")
        proj_in_psum = sem("proj_in_psum")
        proj_ready = sem("proj_ready")
        cols = sem("cols")
        clip_ready = sem("clip_ready")
        exps_ready = sem("exps_ready")
        scale_a_ready = sem("scale_a_ready")
        scale_bc_ready = sem("scale_bc_ready")
        u_ready = sem("u_ready")
        high_ready = [sem(f"high_ready{m}") for m in range(MATS)]
        low_ready = [sem(f"low_ready{m}") for m in range(MATS)]
        s_row_in_psum = sem("s_row_in_psum")
        s_row_ready = sem("s_row_ready")
        adjT_in_psum = sem("adjT_in_psum")
        a_ready = sem("a_ready")
        bc_ready = sem("bc_ready")
        sums_ready = sem("sums_ready")
        sums_read = sem("sums_read")
        z_ready = sem("z_ready")
        attn_ready = sem("attn_ready")
        den_b_ready = sem("den_b_ready")
        den_ready = sem("den_ready")
        rden_ready = sem("rden_ready")
        alpha_ready = sem("alpha_ready")
        xb_gated_ready = sem("xb_gated_ready")
        mix_b_ready = sem("mix_b_ready")
        sig_ready = sem("sig_ready")
        y_ready = sem("y_ready")
        stats_ready = sem("stats_ready")
        mean_var_ready = sem("mean_var_ready")
        var_eps_ready = sem("var_eps_ready")
        rstd_ready = sem("rstd_ready")
        out_ready = sem("out_ready")
        out_stored = [sem(f"out_stored{b}") for b in range(2)]

        def adj_bf16(par, b, t):
            words = adj_raw[:, par, b, :].bitcast(BF16).rearrange("p (m two) -> p m two", two=2)
            return words[:, t * P:(t + 1) * P, 1]

        def is_first(c):
            return isinstance(c, int) and c == 0

        def tp_slot(bank, u):
            return bank[:, :].bitcast(BF16)[:, u * CI:(u + 1) * CI]

        block = ctx.enter_context(nc.Block())

        @block.sync
        def _(sp):
            def load_adj(c, par):
                for b in range(CHUNK_BLOCKS):
                    sp.dma_start(adj_raw[:, par, b, :], adj_v[bass.ds(c * CHUNK_BLOCKS + b, 1), :, :]
                                 .rearrange("q p m -> p (q m)")).then_inc(adj_loaded[par], 16)

            def store_chunk(c):
                for b in range(CHUNK_BLOCKS):
                    sp.wait_ge(out_ready, c * CHUNK_BLOCKS + b + 1)
                    sp.dma_start(out_v[bass.ds(c * CHUNK_BLOCKS + b, 1), :, :].rearrange("q p d -> p (q d)"),
                                 y_out[:, b, :]).then_inc(out_stored[b], 16)

            def step(c, par, load):
                if load:
                    sp.wait_ge(adjT_in_psum, (c + 2) * GROUPS)
                    load_adj(c + 3, 1 - par)
                store_chunk(c)

            def load_x(g):
                sp.dma_start(x_sb[:, g * GROUP:(g + 1) * GROUP, :],
                             x_v[:, g * GROUP:(g + 1) * GROUP, :]).then_inc(x_loaded[g], 16)

            sp.dma_start(w_all[:, FROM_H, :, 0:d], w_sa.rearrange("(k p) n -> p k n", p=P)).then_inc(w_sa_loaded, 16)
            sp.dma_start(a_bc, a_sa[0, :].partition_broadcast(P)).then_inc(a_loaded, 16)
            load_x(0)
            sp.dma_start(w_all[:, FROM_G, :, 0:d], w_gcnb.rearrange("(k p) n -> p k n", p=P)).then_inc(w_loaded, 16)
            for g in range(1, GROUPS):
                load_x(g)
            load_adj(0, 0)
            load_adj(1, 1)
            sp.wait_ge(adjT_in_psum, GROUPS)
            load_adj(2, 0)
            with sp.Fori(0, (CHUNKS - 4) // 2) as k:
                for par in range(2):
                    step(2 * k + par, par, True)
            for c in range(CHUNKS - 4, CHUNKS):
                step(c, c % 2, c + 3 < CHUNKS)
            for b in range(CHUNK_BLOCKS):
                sp.wait_ge(out_stored[b], 16 * CHUNKS)

        @block.tensor
        def _(pe):
            pe.wait_ge(consts_ready, 2)

            def transpose_x(t):
                if t % GROUP == 0:
                    pe.wait_ge(x_loaded[t // GROUP], 16)
                if t >= 2:
                    pe.wait_ge(xT_ready, t - 1)
                for k in range(KH):
                    mm = nc.tensor.transpose(tp_bank[t % 2][:, k * P:(k + 1) * P],
                                             x_sb[:, t, k * P:(k + 1) * P], ident_f[:, :])
                mm.then_inc(xT_in_psum, 1)

            def project(t):
                pe.wait_ge(xT_ready, t + 1)
                for part in (FROM_G, FROM_H):
                    if t:
                        pe.wait_ge(proj_ready, 2 * t - 1 + part)
                    for k in range(KH):
                        mm = nc.tensor.matmul(proj_bank[part][:, 0:RC], xT[:, t % 2, k * P:(k + 1) * P],
                                              w_all[:, part, k, :], start=(k == 0), stop=(k == KH - 1))
                    mm.then_inc(proj_in_psum, 1)

            def spread_s_left(t):
                if t % GROUP == 0 and t:
                    pe.wait_ge(s_row_ready, t // GROUP)
                for k in range(KH):
                    mm = nc.tensor.matmul(s_bank[:, (t % GROUP) * P:(t % GROUP + 1) * P], w_left[:, k, :],
                                          xT[:, t % 2, k * P:(k + 1) * P], start=(k == 0), stop=(k == KH - 1))
                mm.then_inc(s_row_in_psum, 1)

            def transpose_group(c, par, rnd, g, bank):
                if g == 0:
                    pe.wait_ge(adj_loaded[par], 16 * CHUNK_BLOCKS * rnd)
                for u in range(GROUP):
                    for b in range(CHUNK_BLOCKS):
                        mm = nc.tensor.transpose(tp_slot(bank, u)[:, b * P:(b + 1) * P],
                                                 adj_bf16(par, b, g * GROUP + u), ident_b[:, :])
                mm.then_inc(adjT_in_psum, 1)

            def products_a(g):
                pe.wait_ge(a_ready, g + 1)
                for t in range(g * GROUP, (g + 1) * GROUP):
                    pe.wait_ge(high_ready[0], t + 1)
                    pe.wait_ge(low_ready[0], t + 1)
                    for b in range(CHUNK_BLOCKS):
                        for half in range(2):
                            nc.tensor.matmul(acc[b * MATS][:, 0:MC], left[:, 0, 0, t, b * P:(b + 1) * P],
                                             right[:, 0, t, half, :], start=(t == 0 and half == 0),
                                             stop=(t == T - 1 and half == 1))

            transpose_x(0)
            pe.wait_ge(w_loaded, 16 * 3)
            pe.wait_ge(pad_ready, 1)
            for t in range(T):
                if t + 1 < T:
                    transpose_x(t + 1)
                if t == 0:
                    pe.wait_ge(w_vecs_ready, 2 * KH)
                project(t)
                if t == 0:
                    pe.wait_ge(w_left_ready, KH)
                spread_s_left(t)
                g = t // GROUP
                if t % GROUP == GROUP - 1:
                    if g:
                        products_a(g - 1)
                    transpose_group(0, 0, 1, g, adj0_bank)
            products_a(GROUPS - 1)

            def product(c, par, b, m, first):
                for t in range(T):
                    g = t // GROUP
                    if b == 0 and t % GROUP == 0:
                        if m == 0:
                            pe.wait_ge(a_ready, c * GROUPS + g + 1)
                        else:
                            pe.wait_ge(bc_ready, 2 * (c * GROUPS + g) + m)
                    if first:
                        pe.wait_ge(high_ready[m], t + 1)
                        pe.wait_ge(low_ready[m], t + 1)
                    for half in range(2):
                        mm = nc.tensor.matmul(acc[b * MATS + m][:, 0:MC],
                                              left[:, par, m, t, b * P:(b + 1) * P],
                                              right[:, m, t, half, :],
                                              start=(t == 0 and half == 0), stop=(t == T - 1 and half == 1))
                return mm

            def next_group(k, par, g):
                pe.wait_ge(a_ready, (2 * k + par + 1) * GROUPS + g - 1)
                transpose_group(2 * k + par + 1, 1 - par, k + par + 1, g, tp_bank[g % 2])

            def step(k, par, nxt):
                c = 2 * k + par
                for b in range(CHUNK_BLOCKS):
                    for m in range(MATS):
                        if nxt and b * MATS + m < GROUPS:
                            next_group(k, par, b * MATS + m)
                        if m == 0:
                            pe.wait_ge(sums_read, c * CHUNK_BLOCKS + b - 1)
                        mm = product(c, par, b, m, False)
                    mm.then_inc(sums_ready, 1)

            pe.wait_ge(proj_ready, 2 * T)
            pe.wait_ge(s_row_ready, GROUPS)
            for m in range(MATS):
                if m:
                    for b in range(CHUNK_BLOCKS):
                        mm = product(0, 0, b, m, b == 0)
                        if m == MATS - 1:
                            mm.then_inc(sums_ready, 1)
                next_group(0, 0, m)
            next_group(0, 0, GROUPS - 1)
            step(0, 1, True)
            with pe.Fori(1, LOOP_PAIRS) as k:
                for par in range(2):
                    step(k, par, True)
            step(LOOP_PAIRS, 0, True)
            step(LOOP_PAIRS, 1, False)

        @block.scalar
        def _(act):
            for col, row in ((d, wa), (d + 1, wb)):
                act.dma_start(w_all[:, :, :, col:col + 1],
                              row.rearrange("a (s k p) -> p s k a", p=P, k=KH),
                              allow_slow_non_contiguous=True).then_inc(w_loaded, 16)
            act.dma_start(b_bc[:, :], b_gcnb.partition_broadcast(P)).then_inc(small_loaded, 16)
            act.dma_start(gate_b[:, 0:1], ba.partition_broadcast(P)).then_inc(small_loaded, 16)
            act.dma_start(gate_b[:, 1:2], bb.partition_broadcast(P)).then_inc(small_loaded, 16)

            def copy_xT(t):
                act.wait_ge(xT_in_psum, t + 1)
                if t >= 2:
                    act.wait_ge(s_row_in_psum, t - 1)
                nc.scalar.activation(xT[:, t % 2, :], tp_bank[t % 2][:, 0:d], ACT.Copy).then_inc(xT_ready, 1)

            def copy_proj(t):
                for part in (FROM_G, FROM_H):
                    act.wait_ge(proj_in_psum, 2 * t + part + 1)
                    nc.scalar.activation(proj[:, t, part, :], proj_bank[part][:, 0:RC],
                                         ACT.Copy).then_inc(proj_ready, 1)

            def exps(g):
                ts = slice(g * GROUP, (g + 1) * GROUP)
                act.wait_ge(clip_ready, g + 1)
                nc.scalar.activation(p_raw[:, ts], s_clip[:, ts, 1], ACT.Exp, scale=-1.0)
                nc.scalar.activation(p_top[:, ts], s_clip[:, ts, 1], ACT.Exp, scale=-1.0)
                nc.scalar.activation(q_raw[:, ts], proj[:, ts, FROM_H, S_RIGHT], ACT.Exp,
                                     scale=-SLOPE).then_inc(exps_ready, 1)

            def high_a(t):
                act.wait_ge(scale_a_ready, 1)
                nc.scalar.activation(right[:, 0, t, 0, :], proj[:, t, FROM_G, 0:MC], ACT.Copy,
                                     scale=scale[:, 0, t:t + 1]).then_inc(high_ready[0], 1)

            def copy_a(par, t, bank):
                nc.scalar.activation(left[:, par, 0, t, :], tp_slot(bank, t % GROUP), ACT.Copy,
                                     scale=row_pow[:, t:t + 1])
                return nc.scalar.activation(left[:, par, 2, t, :], tp_slot(bank, t % GROUP), ACT.Copy,
                                            scale=left_c[:, t:t + 1])

            def copy_a_first(t):
                g = t // GROUP
                act.wait_ge(scale_bc_ready, g + 1)
                act.wait_ge(adjT_in_psum, g + 1)
                op = copy_a(0, t, adj0_bank)
                if t % GROUP == GROUP - 1:
                    op.then_inc(a_ready, 1)

            def copy_s_row(g):
                act.wait_ge(s_row_in_psum, (g + 1) * GROUP)
                nc.scalar.activation(s_left_row[:, g * 512:(g + 1) * 512], s_bank, ACT.Copy).then_inc(s_row_ready, 1)

            def after(g, u):
                if u == 0:
                    exps(g)
                high_a(g * GROUP + u)
                if u > 0:
                    copy_a_first(g * GROUP + u - 1)
                if u == GROUP - 1:
                    copy_a_first(g * GROUP + u)

            copy_xT(0)
            for t in range(T):
                if t + 1 < T:
                    copy_xT(t + 1)
                copy_proj(t)
                if t % GROUP == GROUP - 1:
                    copy_s_row(t // GROUP)
                if t >= GROUP:
                    after(t // GROUP - 1, t % GROUP)
            for u in range(GROUP):
                after(GROUPS - 1, u)
            nc.scalar.activation(u_raw[:, 0, :], s_clip[:, :, 0], ACT.Exp, scale=-1.0)
            nc.scalar.activation(u_raw[:, 1, :], proj[:, :, FROM_H, S_LEFT], ACT.Exp, scale=-SLOPE).then_inc(u_ready, 1)

            def copy_group(c, par, g, recycled):
                if g == 0 and recycled:
                    act.wait_ge(sums_ready, (c - 1) * CHUNK_BLOCKS)
                act.wait_ge(adjT_in_psum, c * GROUPS + g + 1)
                for u in range(GROUP):
                    op = copy_a(par, g * GROUP + u, tp_bank[g % 2])
                op.then_inc(a_ready, 1)

            def epilogue(c, b):
                q = c * CHUNK_BLOCKS + b
                act.wait_ge(z_ready, q + 1)
                nc.scalar.activation(attn[:, b, :], z[:, b, :], ACT.Sigmoid).then_inc(attn_ready, 1)
                act.wait_ge(attn_ready, q + 1)
                nc.scalar.activation(xb[:, b, :], xb[:, b, :], ACT.Copy,
                                     scale=attn[:, b, 1:2]).then_inc(xb_gated_ready, 1)
                act.wait_ge(sums_read, q + 1)
                nc.scalar.activation(mix[:, b, :], mix[:, b, :], ACT.Sigmoid).then_inc(sig_ready, 1)

            def step(c, par, nxt, recycled=True):
                if nxt:
                    for g in range(GROUPS):
                        copy_group(c + 1, 1 - par, g, recycled)
                for b in range(CHUNK_BLOCKS):
                    epilogue(c, b)

            step(0, 0, True, recycled=False)
            step(1, 1, True)
            with act.Fori(1, LOOP_PAIRS) as k:
                for par in range(2):
                    step(2 * k + par, par, True)
            step(CHUNKS - 2, 0, True)
            step(CHUNKS - 1, 1, False)

        @block.vector
        def _(dve):
            nc.vector.memset(w_all[:, FROM_G, :, d + 2:RC], 0.0).then_inc(pad_ready, 1)
            nc.vector.memset(ones[:, :], 1.0).then_inc(pad_ready, 1)
            dve.wait_ge(a_loaded, 16)
            dve.wait_ge(w_sa_loaded, 16)
            for side in (1, 0):
                for k in range(KH):
                    if k or not side:
                        dve.wait_ge(w_vecs_ready, (1 - side) * KH + k)
                    nc.vector.tensor_tensor_reduce(out=a_prod, in0=w_all[:, FROM_H, k, 0:d],
                                                   in1=a_bc[:, side * d:(side + 1) * d], scale=1.0, scalar=0.0,
                                                   op0=ALU.mult, op1=ALU.add,
                                                   accum_out=w_all[:, FROM_H, k, S_LEFT + side:S_LEFT + side + 1]
                                                   ).then_inc(w_vecs_ready, 1)
            dve.wait_ge(w_vecs_ready, 2 * KH)
            dve.wait_ge(pad_ready, 2)
            for k in range(KH):
                nc.vector.tensor_scalar(w_left[:, k, :], ones[:, :], w_all[:, FROM_H, k, S_LEFT:S_LEFT + 1], None,
                                        ALU.mult).then_inc(w_left_ready, 1)
            dve.wait_ge(w_loaded, 16 * 3)
            nc.vector.tensor_reduce(w_max[:, 0:1], w_all[:, :, :, 0:d + 2].rearrange("p s k c -> p (s k) c"),
                                    mybir.AxisListType.XY, ALU.max, apply_absolute_value=True).then_inc(w_max_part, 1)

            steps = [0]

            def settled(op):
                steps[0] += 1
                op.then_inc(cols, 1)
                dve.wait_ge(cols, steps[0])

            for g in range(GROUPS):
                dve.wait_ge(x_loaded[g], 16)
                op = nc.vector.tensor_reduce(x_max[:, g * GROUP:(g + 1) * GROUP],
                                             x_sb[:, g * GROUP:(g + 1) * GROUP, :], AX_X, ALU.max,
                                             apply_absolute_value=True)
            dve.wait_ge(w_max_ready, 1)
            settled(op)
            settled(nc.vector.tensor_scalar(row_bound[:, :], x_max[:, :], w_max[:, 1:2], float(d), ALU.mult, ALU.mult))
            settled(nc.vector.tensor_scalar(row_top[:, :], row_bound[:, :], 1.0, None, ALU.max))
            settled(nc.vector.tensor_scalar(row_inv[:, :].bitcast(I32), row_top[:, :].bitcast(I32),
                                            EXPONENT, EXPONENT, ALU.bitwise_and, ALU.bitwise_xor))
            nc.vector.tensor_scalar(scale[:, 0, :], row_inv[:, :], ROW_SIZE / 2, None,
                                    ALU.mult).then_inc(scale_a_ready, 1)
            nc.vector.tensor_scalar(row_pow[:, :].bitcast(I32), row_top[:, :].bitcast(I32), EXPONENT, None,
                                    ALU.bitwise_and).then_inc(scale_a_ready, 1)

            def columns(g):
                t0, t1 = g * GROUP, (g + 1) * GROUP
                dve.wait_ge(proj_ready, 2 * t1)
                nc.vector.tensor_scalar(s_clip[:, t0:t1, :], proj[:, t0:t1, FROM_H, S_LEFT:S_RIGHT + 1],
                                        -EXP_ROOM, EXP_ROOM, ALU.max, ALU.min).then_inc(clip_ready, 1)
                nc.vector.tensor_scalar(s_neg[:, t0:t1], proj[:, t0:t1, FROM_H, S_RIGHT], -1.0, None, ALU.mult)
                dve.wait_ge(scale_a_ready, 2)
                dve.wait_ge(exps_ready, g + 1)
                settled(nc.vector.reciprocal(p_rec[:, t0:t1], p_top[:, t0:t1]))
                settled(nc.vector.tensor_tensor(p_rest[:, t0:t1], p_raw[:, t0:t1], p_rec[:, t0:t1], ALU.mult))
                nc.vector.tensor_tensor(left_c[:, t0:t1], row_pow[:, t0:t1], p_top[:, t0:t1], ALU.mult)
                nc.vector.tensor_tensor(scale[:, 1, t0:t1], q_raw[:, t0:t1], scale[:, 0, t0:t1], ALU.mult)
                nc.vector.tensor_tensor(scale[:, 2, t0:t1], p_rest[:, t0:t1], scale[:, 0, t0:t1],
                                        ALU.mult).then_inc(scale_bc_ready, 1)
                dve.wait_ge(scale_bc_ready, g + 1)
                settled(nc.vector.tensor_copy(right[:, 1:3, t0:t1, 0, d], scale[:, 1:3, t0:t1]))
                nc.vector.tensor_tensor(right[:, 1:3, t0:t1, 1, d], scale[:, 1:3, t0:t1],
                                        right[:, 1:3, t0:t1, 0, d], ALU.subtract)

            def low(m, t):
                part, width = (FROM_G, MC) if m == 0 else (FROM_H, d)
                dve.wait_ge(high_ready[m], t + 1)
                nc.vector.scalar_tensor_tensor(out=right[:, m, t, 1, 0:width], in0=proj[:, t, part, 0:width],
                                               scalar=scale[:, m, t:t + 1], in1=right[:, m, t, 0, 0:width],
                                               op0=ALU.mult, op1=ALU.subtract).then_inc(low_ready[m], 1)

            def gate_group(c, par, g, recycled=True):
                if g == 0 and recycled:
                    dve.wait_ge(sums_ready, (c - 1) * CHUNK_BLOCKS)
                dve.wait_ge(a_ready, c * GROUPS + g + 1)
                s_row = s_left_row[:, bass.ds(c * CI, CI)]
                for m, src, cmp in ((1, 0, ALU.is_lt), (2, 2, ALU.is_ge)):
                    for u in range(GROUP):
                        t = g * GROUP + u
                        op = nc.vector.scalar_tensor_tensor(out=left[:, par, m, t, :], in0=s_row,
                                                            scalar=s_neg[:, t:t + 1], in1=left[:, par, src, t, :],
                                                            op0=cmp, op1=ALU.mult)
                    op.then_inc(bc_ready, 1)

            def epilogue(c, b):
                q = c * CHUNK_BLOCKS + b
                acc_a, acc_b, acc_c = acc[b * MATS:(b + 1) * MATS]
                dve.wait_ge(sums_ready, q + 1)
                uv_q = uv[:, bass.ds(q, 1), :].rearrange("p q s -> p (q s)")
                gate_q = gate_x[:, bass.ds(q, 1), :].rearrange("p q s -> p (q s)")
                nc.vector.scalar_tensor_tensor(out=z[:, b, :], in0=acc_a[:, d:d + 2], scalar=1.0 / ROW_SIZE,
                                               in1=gate_q, op0=ALU.mult, op1=ALU.add)
                nc.vector.tensor_tensor(den_b[:, b, :], acc_b[:, d:d + 1], uv_q[:, 1:2],
                                        ALU.mult).then_inc(den_b_ready, 1)
                nc.vector.scalar_tensor_tensor(out=xb[:, b, :], in0=acc_a[:, 0:d], scalar=1.0 / ROW_SIZE,
                                               in1=b_bc[:, :], op0=ALU.mult, op1=ALU.add).then_inc(z_ready, 1)
                dve.wait_ge(den_b_ready, q + 1)
                nc.vector.scalar_tensor_tensor(out=den[:, b, :], in0=acc_c[:, d:d + 1], scalar=uv_q[:, 0:1],
                                               in1=den_b[:, b, :], op0=ALU.mult, op1=ALU.add).then_inc(den_ready, 1)
                dve.wait_ge(den_ready, 2 * q + 1)
                nc.vector.tensor_scalar(den[:, b, :], den[:, b, :], DEN_EPS, None, ALU.add).then_inc(den_ready, 1)
                dve.wait_ge(den_ready, 2 * q + 2)
                nc.vector.reciprocal(rden[:, b, :], den[:, b, :]).then_inc(rden_ready, 1)
                dve.wait_ge(rden_ready, q + 1)
                dve.wait_ge(attn_ready, q + 1)
                nc.vector.tensor_scalar(alpha[:, b, :], uv_q, rden[:, b, :], attn[:, b, 0:1], ALU.mult,
                                        ALU.mult).then_inc(alpha_ready, 1)
                dve.wait_ge(alpha_ready, q + 1)
                dve.wait_ge(xb_gated_ready, q + 1)
                nc.vector.scalar_tensor_tensor(out=mix[:, b, :], in0=acc_b[:, 0:d], scalar=alpha[:, b, 1:2],
                                               in1=xb[:, b, :], op0=ALU.mult,
                                               op1=ALU.add).then_inc(mix_b_ready, 1)
                dve.wait_ge(mix_b_ready, q + 1)
                nc.vector.scalar_tensor_tensor(out=mix[:, b, :], in0=acc_c[:, 0:d], scalar=alpha[:, b, 0:1],
                                               in1=mix[:, b, :], op0=ALU.mult, op1=ALU.add).then_inc(sums_read, 1)
                dve.wait_ge(y_ready, q + 1)
                nc.vector.bn_stats(stats[:, b, :], y[:, b, :]).then_inc(stats_ready, 1)
                if b > 0 or not is_first(c):
                    normalise(c, b - 1) if b > 0 else normalise(c - 1, CHUNK_BLOCKS - 1)
                else:
                    dve.wait_ge(stats_ready, q + 1)
                nc.vector.bn_aggr(mean_var[:, b, :], stats[:, b, :]).then_inc(mean_var_ready, 1)
                dve.wait_ge(mean_var_ready, q + 1)
                nc.vector.tensor_scalar(var_eps[:, b, :], mean_var[:, b, 1:2], LN_EPS, None,
                                        ALU.add).then_inc(var_eps_ready, 1)

            def normalise(c, b, more=True):
                q = c * CHUNK_BLOCKS + b
                if more:
                    dve.wait_ge(stats_ready, q + 2)
                dve.wait_ge(rstd_ready, q + 1)
                if not is_first(c):
                    dve.wait_ge(out_stored[b], 16 * c)
                nc.vector.tensor_scalar(y_out[:, b, :], y[:, b, :], mean_var[:, b, 0:1], rstd[:, b, :],
                                        ALU.subtract, ALU.mult).then_inc(out_ready, 1)

            def step(c, par, nxt, recycled=True):
                if nxt:
                    for g in range(GROUPS):
                        gate_group(c + 1, 1 - par, g, recycled)
                for b in range(CHUNK_BLOCKS):
                    epilogue(c, b)

            nc.vector.memset(right[:, 1:3, :, :, d + 1:d + 2], 0.0)
            for g in range(GROUPS):
                columns(g)
                for m in range(MATS):
                    for t in range(g * GROUP, (g + 1) * GROUP):
                        low(m, t)
                if g == 1:
                    dve.wait_ge(s_row_ready, 1)
                if g:
                    gate_group(0, 0, g - 1, recycled=False)
            gate_group(0, 0, GROUPS - 1, recycled=False)
            dve.wait_ge(u_ready, 1)
            dve.wait_ge(small_loaded, 16 * 3)
            nc.vector.tensor_scalar(uv[:, :, :], u_raw[:, :, :].rearrange("p s t -> p t s"), 1.0 / ROW_SIZE, None,
                                    ALU.mult).then_inc(cols, 1)
            for s in range(2):
                nc.vector.tensor_scalar(gate_x[:, :, s:s + 1], proj[:, :, FROM_H, d + s:d + s + 1],
                                        gate_b[:, s:s + 1], None, ALU.add).then_inc(cols, 1)
            dve.wait_ge(cols, steps[0] + 3)
            dve.wait_ge(s_row_ready, GROUPS)
            step(0, 0, True, recycled=False)
            step(1, 1, True)
            with dve.Fori(1, LOOP_PAIRS) as k:
                for par in range(2):
                    step(2 * k + par, par, True)
            step(CHUNKS - 2, 0, True)
            step(CHUNKS - 1, 1, False)
            normalise(CHUNKS - 1, CHUNK_BLOCKS - 1, more=False)

        @block.gpsimd
        def _(pool):
            nc.gpsimd.memset(ident_f[:, :], 0.0).then_inc(consts_zeroed, 1)
            nc.gpsimd.memset(ident_b[:, :], 0.0).then_inc(consts_zeroed, 1)
            nc.gpsimd.memset(minus_half[:, :], -0.5)
            pool.wait_ge(consts_zeroed, 2)
            for m in (ident_f, ident_b):
                nc.gpsimd.affine_select(out=m[:, :], in_=m[:, :], compare_op=ALU.not_equal, fill=1.0, base=0,
                                        pattern=[[-1, P]], channel_multiplier=1).then_inc(consts_ready, 1)

            def high(m, t):
                nc.gpsimd.tensor_tensor(right[:, m, t, 0, 0:d], proj[:, t, FROM_H, 0:d],
                                        scale[:, m, t:t + 1].to_broadcast([P, d]), ALU.mult).then_inc(high_ready[m], 1)

            pool.wait_ge(w_max_part, 1)
            nc.gpsimd.partition_all_reduce(w_max[:, 1:2], w_max[:, 0:1], P, bass.bass_isa.ReduceOp.max
                                           ).then_inc(w_max_ready, 1)

            for g in range(GROUPS):
                pool.wait_ge(scale_bc_ready, g + 1)
                for m in (1, 2):
                    for t in range(g * GROUP, (g + 1) * GROUP):
                        high(m, t)

            def finish(c, b, recycled):
                q = c * CHUNK_BLOCKS + b
                pool.wait_ge(sig_ready, q + 1)
                if recycled:
                    pool.wait_ge(out_ready, q - 1)
                nc.gpsimd.tensor_tensor(y[:, b, :], x_sb[:, bass.ds(q, 1), :].rearrange("p q d -> p (q d)"),
                                        mix[:, b, :], ALU.add).then_inc(y_ready, 1)
                pool.wait_ge(var_eps_ready, q + 1)
                nc.gpsimd.tensor_tensor(rstd[:, b, :], var_eps[:, b, :], minus_half[:, :],
                                        ALU.pow).then_inc(rstd_ready, 1)

            for b in range(CHUNK_BLOCKS):
                finish(0, b, False)
            with pool.Fori(1, CHUNKS) as c:
                for b in range(CHUNK_BLOCKS):
                    finish(c, b, True)


_INS = ["x", "adj", "L0_gnn_W_sa", "L0_gnn_a_sa", "L0_gnn_W_gcnb", "L0_gnn_b_gcnb",
        "L0_gnn_Wa", "L0_gnn_ba", "L0_gnn_Wb", "L0_gnn_bb"]


def kernel(**inputs):
    import numpy as _np
    import concourse.bacc as _bacc
    from concourse import mybir as _mybir
    from concourse.bass_utils import run_bass_kernel_spmd as _run

    nc = _bacc.Bacc("TRN2", target_bir_lowering=False, num_devices=1)
    arrays, args = {}, []
    for name in _INS:
        a = _np.ascontiguousarray(inputs[name])
        arrays[f"in_{name}_dram"] = a
        args.append(nc.dram_tensor(f"in_{name}_dram", a.shape, _mybir.dt.from_np(a.dtype), kind="ExternalInput").ap())
    o = nc.dram_tensor("out_dram", tuple(inputs["x"].shape), _mybir.dt.float32, kind="ExternalOutput").ap()
    build(nc, *args, o)
    r = _run(nc, [arrays], core_ids=[0])
    return r.results[0]["out_dram"]
```

```python
from contextlib import ExitStack

import concourse.bass as bass
from concourse import mybir

P = 128
F32 = mybir.dt.float32
BF16 = mybir.dt.bfloat16
FP16 = mybir.dt.float16
F32R = mybir.dt.float32r
I32 = mybir.dt.int32
ALU = mybir.AluOpType
ACT = mybir.ActivationFunctionType
AX_X = mybir.AxisListType.X

SLOPE = 0.01
DEN_EPS = 1e-5
LN_EPS = 1e-5
EXP_ROOM = 80.0
ROW_SIZE = 8192.0
EXPONENT = 0x7F800000
TOP_12 = -(1 << 12)

CHUNK_BLOCKS = 2
GROUP = 4


def build(nc, x, adj, w_sa, a_sa, w_gcnb, b_gcnb, wa, ba, wb, bb, out):
    n, d = x.shape
    T = n // P
    KH = d // P
    CI = CHUNK_BLOCKS * P
    CHUNKS = n // CI
    GROUPS = T // GROUP
    RC = d + 4
    MC = d + 2
    FROM_G, FROM_H = 0, 1
    S_LEFT, S_RIGHT = d + 2, d + 3
    LOOP_PAIRS = (CHUNKS - 2) // 2
    MATS = 3

    x_v = x.rearrange("(t p) d -> p t d", p=P)
    adj_v = adj.rearrange("(q p) m -> q p m", p=P)
    out_v = out.rearrange("(q p) d -> q p d", p=P)

    with ExitStack() as ctx:
        def sb(name, shape, dt):
            return ctx.enter_context(nc.sbuf_tensor(name, shape, dt))

        def sem(name):
            return ctx.enter_context(nc.semaphore(name))

        def sb_before(name, shape, dt):
            with nc.sbuf_tensor(name, shape, dt) as buf:
                return buf

        x_sb = sb("x_sb", [P, T, d], F32)
        adj_raw = sb("adj_raw", [P, 2, CHUNK_BLOCKS, n], F32)
        left = sb("left", [P, 2, MATS, T, CI], BF16)
        x_parts = sb_before("x_parts", [P, MATS, T, MC], F32R)[:, 1:3, :, 0:d]
        right = sb("right", [P, MATS, T, 2, MC], FP16)
        s_left_row = sb("s_left_row", [P, n], F32)
        proj = sb("proj", [P, T, 2, RC], F32)
        b_bc = sb("b_bc", [P, d], F32)
        gate_b = sb("gate_b", [P, 2], F32)
        w_parts = sb("w_parts", [P, 2, 2, KH, RC], F32R)
        ident_f = sb("ident_f", [P, P], F32)
        ident_b = sb("ident_b", [P, P], BF16)
        ident_r = sb("ident_r", [P, P], F32R)
        w_max = sb("w_max", [P, 2], F32)
        x_size = sb("x_size", [P, T], F32)
        row_bound = sb("row_bound", [P, T], F32)
        row_top = sb("row_top", [P, T], F32)
        row_pow = sb("row_pow", [P, T], F32)
        row_inv = sb("row_inv", [P, T], F32)
        s_clip = sb("s_clip", [P, T, 2], F32)
        s_neg = sb("s_neg", [P, T], F32)
        u_raw = sb("u_raw", [P, 2, T], F32)
        q_raw = sb("q_raw", [P, T], F32)
        p_raw = sb("p_raw", [P, T], F32)
        p_top = sb("p_top", [P, T], BF16)
        p_top_f = sb("p_top_f", [P, T], F32)
        p_rec = sb("p_rec", [P, T], F32)
        p_rest = sb("p_rest", [P, T], F32)
        scale = sb("scale", [P, MATS, T], F32)
        uv = sb("uv", [P, T, 2], F32)
        gate_x = sb("gate_x", [P, T, 2], F32)
        z = sb("z", [P, 2, 2], F32)
        attn = sb("attn", [P, 2, 2], F32)
        den_b = sb("den_b", [P, 2, 1], F32)
        den = sb("den", [P, 2, 1], F32)
        rden = sb("rden", [P, 2, 1], F32)
        alpha = sb("alpha", [P, 2, 2], F32)
        mixed = sb("mixed", [P, 2, 2, d], F32)
        xb, mix = mixed[:, 0, :, :], mixed[:, 1, :, :]
        xT = sb_before("xT", [P, 2, 2, d], F32R)
        y_both = sb("y_both", [P, 2, 2, d], F32)
        y, y_out = y_both[:, 0, :, :], y_both[:, 1, :, :]
        stats = sb("stats", [P, 2, 6], F32)
        mean_var = sb("mean_var", [P, 2, 2], F32)
        var_eps = sb("var_eps", [P, 2, 1], F32)
        minus_half = sb("minus_half", [P, 1], F32)
        rstd = sb("rstd", [P, 2, 1], F32)

        W_SIZE = 2 * KH * RC
        w_all = s_left_row[:, 0:W_SIZE].rearrange("p (s k c) -> p s k c", s=2, k=KH)
        a_bc = s_left_row[:, W_SIZE:W_SIZE + 2 * d]
        a_prod = s_left_row[:, W_SIZE + 2 * d:W_SIZE + 3 * d]
        w_top = mixed[:, :, :, :].rearrange("p s b d -> p (s b d)").bitcast(I32)
        x_top = right[:, 2, :, :, :].bitcast(I32).rearrange("p t h c -> p t (h c)")[:, :, 0:d]

        tp_bank = [ctx.enter_context(nc.psum_tensor(f"tp_bank{i}", [P, 512], F32)) for i in range(2)]
        sums = ctx.enter_context(nc.psum_tensor("sums", [P, 2 * MATS, 512], F32))
        acc = [sums[:, i, :] for i in range(2 * MATS)]
        x_bank = tp_bank[0]
        proj_bank = [acc[1], acc[2]]
        first_bank = [acc[4], tp_bank[1]]
        s_bank = acc[5]

        w_loaded = sem("w_loaded")
        w_sa_loaded = sem("w_sa_loaded")
        a_loaded = sem("a_loaded")
        small_loaded = sem("small_loaded")
        x_loaded = [sem(f"x_loaded{g}") for g in range(GROUPS)]
        adj_loaded = [sem(f"adj_loaded{i}") for i in range(2)]
        consts_zeroed = sem("consts_zeroed")
        consts_ready = sem("consts_ready")
        w_masked = sem("w_masked")
        x_masked = sem("x_masked")
        w_hi_ready = sem("w_hi_ready")
        w_lo_ready = sem("w_lo_ready")
        w_lo_h_ready = sem("w_lo_h_ready")
        x_hi_ready = sem("x_hi_ready")
        x_lo_ready = sem("x_lo_ready")
        x_sizes_ready = sem("x_sizes_ready")
        w_max_part = sem("w_max_part")
        w_max_ready = sem("w_max_ready")
        w_vecs_ready = sem("w_vecs_ready")
        xT_in_psum = sem("xT_in_psum")
        xT_ready = sem("xT_ready")
        proj_in_psum = sem("proj_in_psum")
        proj_ready = sem("proj_ready")
        cols = sem("cols")
        clip_ready = sem("clip_ready")
        exps_ready = sem("exps_ready")
        scale_a_ready = sem("scale_a_ready")
        scale_bc_ready = sem("scale_bc_ready")
        u_ready = sem("u_ready")
        high_ready = [sem(f"high_ready{m}") for m in range(MATS)]
        low_ready = [sem(f"low_ready{m}") for m in range(MATS)]
        s_row_in_psum = sem("s_row_in_psum")
        s_row_ready = sem("s_row_ready")
        adjT_in_psum = sem("adjT_in_psum")
        a_ready = sem("a_ready")
        b_ready = sem("b_ready")
        rest_ready = sem("rest_ready")
        c_ready = sem("c_ready")
        first_c_ready = sem("first_c_ready")
        a_sums_ready = sem("a_sums_ready")
        sums_ready = sem("sums_ready")
        last_b_ready = sem("last_b_ready")
        last_mix_b_ready = sem("last_mix_b_ready")
        last_mix_c_ready = sem("last_mix_c_ready")
        sums_read = sem("sums_read")
        z_ready = sem("z_ready")
        rows_0_1_loaded = sem("rows_0_1_loaded")
        attn_ready = sem("attn_ready")
        den_b_ready = sem("den_b_ready")
        den_ready = sem("den_ready")
        rden_ready = sem("rden_ready")
        alpha_ready = sem("alpha_ready")
        xb_gated_ready = sem("xb_gated_ready")
        mix_b_ready = sem("mix_b_ready")
        sig_ready = sem("sig_ready")
        y_ready = sem("y_ready")
        stats_ready = sem("stats_ready")
        mean_var_ready = sem("mean_var_ready")
        var_eps_ready = sem("var_eps_ready")
        rstd_ready = sem("rstd_ready")
        out_ready = sem("out_ready")
        out_stored = [sem(f"out_stored{b}") for b in range(2)]

        def adj_bf16(par, b, t):
            words = adj_raw[:, par, b, :].bitcast(BF16).rearrange("p (m two) -> p m two", two=2)
            return words[:, t * P:(t + 1) * P, 1]

        FIRST_C = 2
        SIZED = GROUP

        def turn(t, part):
            return 2 * part + t + 1 if t < 2 else 2 * t + part + 1

        FIRST_AT = [4, 7, 9, 12]

        def is_first(c):
            return isinstance(c, int) and c == 0

        def tp_slot(bank, u):
            return bank[:, :].bitcast(BF16)[:, u * CI:(u + 1) * CI]

        block = ctx.enter_context(nc.Block())

        @block.sync
        def _(sp):
            def load_adj(c, par):
                for b in range(CHUNK_BLOCKS):
                    sp.dma_start(adj_raw[:, par, b, :], adj_v[bass.ds(c * CHUNK_BLOCKS + b, 1), :, :]
                                 .rearrange("q p m -> p (q m)")).then_inc(adj_loaded[par], 16)

            def store_chunk(c):
                for b in range(CHUNK_BLOCKS):
                    sp.wait_ge(out_ready, c * CHUNK_BLOCKS + b + 1)
                    sp.dma_start(out_v[bass.ds(c * CHUNK_BLOCKS + b, 1), :, :].rearrange("q p d -> p (q d)"),
                                 y_out[:, b, :]).then_inc(out_stored[b], 16)

            def step(c, par, load):
                if load:
                    sp.wait_ge(adjT_in_psum, (c + 2) * GROUPS)
                    load_adj(c + 3, 1 - par)
                store_chunk(c)

            def load_x(t0, t1, done):
                sp.dma_start(x_sb[:, t0:t1, :], x_v[:, t0:t1, :]).then_inc(done, 16)

            load_x(0, 2, rows_0_1_loaded)
            sp.dma_start(w_all[:, FROM_G, :, 0:d], w_gcnb.rearrange("(k p) n -> p k n", p=P)).then_inc(w_loaded, 16)
            sp.dma_start(w_all[:, FROM_H, :, 0:d], w_sa.rearrange("(k p) n -> p k n", p=P)).then_inc(w_sa_loaded, 16)
            sp.dma_start(a_bc, a_sa[0, :].partition_broadcast(P)).then_inc(a_loaded, 16)
            load_x(2, GROUP, x_loaded[0])
            for g in range(1, GROUPS):
                load_x(g * GROUP, (g + 1) * GROUP, x_loaded[g])
            sp.dma_start(b_bc[:, :], b_gcnb.partition_broadcast(P)).then_inc(small_loaded, 16)
            sp.dma_start(gate_b[:, 0:1], ba.partition_broadcast(P)).then_inc(small_loaded, 16)
            sp.dma_start(gate_b[:, 1:2], bb.partition_broadcast(P)).then_inc(small_loaded, 16)
            load_adj(0, 0)
            load_adj(1, 1)
            sp.wait_ge(adjT_in_psum, GROUPS)
            load_adj(2, 0)
            with sp.Fori(0, (CHUNKS - 4) // 2) as k:
                for par in range(2):
                    step(2 * k + par, par, True)
            for c in range(CHUNKS - 4, CHUNKS):
                step(c, c % 2, c + 3 < CHUNKS)
            for b in range(CHUNK_BLOCKS):
                sp.wait_ge(out_stored[b], 16 * CHUNKS)

        @block.tensor
        def _(pe):
            pe.wait_ge(consts_ready, 3)

            def transpose_x(t):
                pe.wait_ge(x_hi_ready, 1 if t < 2 else t // GROUP + 2)
                pe.wait_ge(x_lo_ready, t + 1)
                if t:
                    pe.wait_ge(xT_ready, t)
                for part in range(2):
                    for k in range(KH):
                        mm = nc.tensor.transpose(x_bank[:, part * d + k * P:part * d + (k + 1) * P].bitcast(F32R),
                                                 x_parts[:, part, t, k * P:(k + 1) * P], ident_r[:, :])
                mm.then_inc(xT_in_psum, 1)

            def project(t, part):
                if part == FROM_G:
                    pe.wait_ge(xT_ready, t + 1)
                if t == 0:
                    pe.wait_ge(w_hi_ready, 1 if part == FROM_G else 3)
                    pe.wait_ge(w_lo_ready, 1 if part == FROM_G else 2)
                    if part == FROM_H:
                        pe.wait_ge(w_lo_h_ready, 1)
                else:
                    pe.wait_ge(proj_ready, turn(t - 1, part))
                width = (MC, RC)[part]
                for k in range(KH):
                    for of_x, of_w in ((0, 0), (0, 1), (1, 0)):
                        mm = nc.tensor.matmul(proj_bank[part][:, 0:width], xT[:, t % 2, of_x, k * P:(k + 1) * P],
                                              w_parts[:, part, of_w, k, 0:width], start=(k == 0 and of_x == of_w),
                                              stop=(k == KH - 1 and of_x == 1))
                mm.then_inc(proj_in_psum, 1)

            def spread_s_left(g):
                pe.wait_ge(proj_ready, 2 * (g + 1) * GROUP)
                if g:
                    pe.wait_ge(s_row_ready, g)
                for u in range(GROUP):
                    mm = nc.tensor.transpose(s_bank[:, u * P:(u + 1) * P],
                                             proj[:, g * GROUP + u, FROM_H, S_LEFT:S_LEFT + 1].to_broadcast([P, P]),
                                             ident_f[:, :])
                mm.then_inc(s_row_in_psum, 1)

            def transpose_group(c, par, rnd, g, bank):
                if g == 0:
                    pe.wait_ge(adj_loaded[par], 16 * CHUNK_BLOCKS * rnd)
                for u in range(GROUP):
                    for b in range(CHUNK_BLOCKS):
                        mm = nc.tensor.transpose(tp_slot(bank, u)[:, b * P:(b + 1) * P],
                                                 adj_bf16(par, b, g * GROUP + u), ident_b[:, :])
                mm.then_inc(adjT_in_psum, 1)

            def products_a(g):
                pe.wait_ge(a_ready, g + 1)
                for t in range(g * GROUP, (g + 1) * GROUP):
                    pe.wait_ge(high_ready[0], t + 1)
                    pe.wait_ge(low_ready[0], t + 1)
                    for b in range(CHUNK_BLOCKS):
                        for half in range(2):
                            mm = nc.tensor.matmul(acc[b * MATS][:, 0:MC], left[:, 0, 0, t, b * P:(b + 1) * P],
                                                  right[:, 0, t, half, :], start=(t == 0 and half == 0),
                                                  stop=(t == T - 1 and half == 1))
                if g == GROUPS - 1:
                    mm.then_inc(a_sums_ready, CHUNK_BLOCKS)

            def first_group(g):
                if g >= 2:
                    pe.wait_ge(a_ready, g - 1)
                transpose_group(0, 0, 1, g, first_bank[g % 2])

            transpose_x(0)
            transpose_x(1)
            project(0, FROM_G)
            project(1, FROM_G)
            project(0, FROM_H)
            transpose_x(2)
            project(1, FROM_H)
            for t in range(2, T):
                if t + 1 < T:
                    transpose_x(t + 1)
                project(t, FROM_G)
                project(t, FROM_H)
                g = t // GROUP - 1
                if t in FIRST_AT:
                    first_group(FIRST_AT.index(t))
                if g >= 0 and t % GROUP == 1:
                    spread_s_left(g)
                if g >= 1 and t % GROUP == 2:
                    products_a(g - 1)
            spread_s_left(GROUPS - 1)
            products_a(GROUPS - 2)

            def product(c, par, b, m, first):
                for t in range(T):
                    g = t // GROUP
                    if b == 0 and t % GROUP == 0:
                        if is_first(c) and m == 2 and g < FIRST_C:
                            pe.wait_ge(first_c_ready, g + 1)
                        else:
                            pe.wait_ge((a_ready, b_ready, c_ready)[m], c * GROUPS + g + 1)
                    if first:
                        pe.wait_ge(high_ready[m], t + 1)
                        pe.wait_ge(low_ready[m], t + 1)
                    for half in range(2):
                        mm = nc.tensor.matmul(acc[b * MATS + m][:, 0:MC],
                                              left[:, par, m, t, b * P:(b + 1) * P],
                                              right[:, m, t, half, :],
                                              start=(t == 0 and half == 0), stop=(t == T - 1 and half == 1))
                if m == 0:
                    mm.then_inc(a_sums_ready, 1)
                if m == 1 and b == CHUNK_BLOCKS - 1 and isinstance(c, int) and c == CHUNKS - 1:
                    mm.then_inc(last_b_ready, 1)
                if m == MATS - 1:
                    mm.then_inc(sums_ready, 1)

            def next_group(k, par, g):
                pe.wait_ge(a_ready, (2 * k + par + 1) * GROUPS + g - 1)
                transpose_group(2 * k + par + 1, 1 - par, k + par + 1, g, tp_bank[g % 2])

            def step(k, par, nxt):
                c = 2 * k + par
                for b in range(CHUNK_BLOCKS):
                    for m in range(MATS):
                        if nxt and b * MATS + m < GROUPS:
                            next_group(k, par, b * MATS + m)
                        if m == 0:
                            pe.wait_ge(sums_read, c * CHUNK_BLOCKS + b - 1)
                        product(c, par, b, m, False)

            next_group(0, 0, 0)
            products_a(GROUPS - 1)
            pe.wait_ge(proj_ready, 2 * T)
            for m in (1, 2):
                for b in range(CHUNK_BLOCKS):
                    if (m, b) != (1, 0):
                        next_group(0, 0, (m - 1) * CHUNK_BLOCKS + b)
                    if (m, b) == (1, 1):
                        pe.wait_ge(s_row_ready, GROUPS)
                    product(0, 0, b, m, b == 0)
            step(0, 1, True)
            with pe.Fori(1, LOOP_PAIRS) as k:
                for par in range(2):
                    step(k, par, True)
            step(LOOP_PAIRS, 0, True)
            step(LOOP_PAIRS, 1, False)

        @block.scalar
        def _(act):
            for col, row in ((d, wa), (d + 1, wb)):
                act.dma_start(w_all[:, :, :, col:col + 1],
                              row.rearrange("a (s k p) -> p s k a", p=P, k=KH),
                              allow_slow_non_contiguous=True).then_inc(w_loaded, 16)

            def copy_xT(t):
                act.wait_ge(xT_in_psum, t + 1)
                if t >= 2:
                    act.wait_ge(proj_in_psum, turn(t - 2, FROM_H))
                nc.scalar.activation(xT[:, t % 2, :, :].rearrange("p h d -> p (h d)"), x_bank[:, :],
                                     ACT.Copy).then_inc(xT_ready, 1)

            def copy_proj(t, part):
                act.wait_ge(proj_in_psum, turn(t, part))
                width = (MC, RC)[part]
                nc.scalar.activation(proj[:, t, part, 0:width], proj_bank[part][:, 0:width],
                                     ACT.Copy).then_inc(proj_ready, 1)

            def exps(g):
                ts = slice(g * GROUP, (g + 1) * GROUP)
                act.wait_ge(clip_ready, g + 1)
                nc.scalar.activation(p_raw[:, ts], s_clip[:, ts, 1], ACT.Exp, scale=-1.0)
                nc.scalar.activation(p_top[:, ts], s_clip[:, ts, 1], ACT.Exp, scale=-1.0)
                nc.scalar.activation(q_raw[:, ts], proj[:, ts, FROM_H, S_RIGHT], ACT.Exp,
                                     scale=-SLOPE).then_inc(exps_ready, 1)

            def high_a(t):
                act.wait_ge(scale_a_ready, 1)
                act.wait_ge(proj_ready, 2 * t + 1)
                nc.scalar.activation(right[:, 0, t, 0, :], proj[:, t, FROM_G, 0:MC], ACT.Copy,
                                     scale=scale[:, 0, t:t + 1]).then_inc(high_ready[0], 1)

            def copy_a(par, t, bank):
                return nc.scalar.activation(left[:, par, 0, t, :], tp_slot(bank, t % GROUP), ACT.Copy,
                                            scale=row_pow[:, t:t + 1])

            def scale_c(c, par, g, count=1):
                act.wait_ge(rest_ready, c * GROUPS + g + 1)
                for t in range(g * GROUP, (g + 1) * GROUP):
                    op = nc.scalar.activation(left[:, par, 2, t, :], left[:, par, 2, t, :], ACT.Copy,
                                              scale=p_top_f[:, t:t + 1])
                op.then_inc(c_ready, count)

            def copy_first_a(t):
                act.wait_ge(scale_a_ready, 2)
                act.wait_ge(adjT_in_psum, t // GROUP + 1)
                a = copy_a(0, t, first_bank[t // GROUP % 2])
                if t % GROUP == GROUP - 1:
                    a.then_inc(a_ready, 1)

            def copy_s_row(g):
                act.wait_ge(s_row_in_psum, g + 1)
                if g == 0:
                    act.wait_ge(w_max_part, 1)
                nc.scalar.activation(s_left_row[:, g * 512:(g + 1) * 512], s_bank, ACT.Copy).then_inc(s_row_ready, 1)

            def after(g, u):
                t0 = g * GROUP
                if u == min(g, 1) and g < GROUPS - 1:
                    exps(g)
                high_a(t0 + u)

            def size_of_x(t):
                if t < 2:
                    act.wait_ge(rows_0_1_loaded, 16)
                elif t == 2:
                    act.wait_ge(x_loaded[0], 16)
                nc.scalar.activation(left[:, 1, 0, t, 0:d], x_sb[:, t, :], ACT.Abs,
                                     accum_out=x_size[:, t:t + 1]).then_inc(x_sizes_ready, 1)

            copy_xT(0)
            copy_xT(1)
            for part in (FROM_G, FROM_H):
                for t in range(2):
                    size_of_x(2 * part + t)
                    copy_proj(t, part)
                    if (t, part) == (0, FROM_H):
                        copy_xT(2)
            for t in range(2, T):
                if t + 1 < T:
                    copy_xT(t + 1)
                copy_proj(t, FROM_G)
                copy_proj(t, FROM_H)
                if t % GROUP == 2 and t >= GROUP:
                    copy_s_row(t // GROUP - 1)
                if t >= GROUP:
                    after(t // GROUP - 1, t % GROUP)
                for g in range(GROUPS):
                    if t in (FIRST_AT[g] + 1, FIRST_AT[g] + 2):
                        half = 2 * (t - FIRST_AT[g] - 1)
                        copy_first_a(g * GROUP + half)
                        copy_first_a(g * GROUP + half + 1)
            exps(GROUPS - 1)
            for u in range(GROUP):
                after(GROUPS - 1, u)
            copy_s_row(GROUPS - 1)
            nc.scalar.activation(u_raw[:, 0, :], s_clip[:, :, 0], ACT.Exp, scale=-1.0)
            nc.scalar.activation(u_raw[:, 1, :], proj[:, :, FROM_H, S_LEFT], ACT.Exp, scale=-SLOPE).then_inc(u_ready, 1)

            def copy_group(c, par, g):
                if g == 0 and not (isinstance(c, int) and c < 2):
                    act.wait_ge(sums_ready, (c - 1) * CHUNK_BLOCKS)
                act.wait_ge(adjT_in_psum, c * GROUPS + g + 1)
                for u in range(GROUP):
                    a = copy_a(par, g * GROUP + u, tp_bank[g % 2])
                a.then_inc(a_ready, 1)

            def gate_ab(c, b):
                q = c * CHUNK_BLOCKS + b
                act.wait_ge(z_ready, q + 1)
                nc.scalar.activation(attn[:, b, :], z[:, b, :], ACT.Sigmoid).then_inc(attn_ready, 1)
                act.wait_ge(attn_ready, q + 1)
                nc.scalar.activation(xb[:, b, :], xb[:, b, :], ACT.Copy,
                                     scale=attn[:, b, 1:2]).then_inc(xb_gated_ready, 1)

            def squash(c, b):
                q = c * CHUNK_BLOCKS + b
                act.wait_ge(sums_read, q + 1)
                nc.scalar.activation(mix[:, b, :], mix[:, b, :], ACT.Sigmoid).then_inc(sig_ready, 1)

            def step(c, par, nxt):
                def copy(g):
                    if nxt:
                        copy_group(c + 1, 1 - par, g)

                def scale(g):
                    if nxt:
                        scale_c(c + 1, 1 - par, g)

                copy(0)
                squash(c - 1, 1)
                copy(1)
                scale(0)
                gate_ab(c, 0)
                copy(2)
                scale(1)
                copy(3)
                scale(2)
                squash(c, 0)
                scale(3)
                gate_ab(c, 1)

            copy_group(1, 1, 0)
            for g in range(FIRST_C, GROUPS):
                scale_c(0, 0, g, FIRST_C + 1 if g == FIRST_C else 1)
            copy_group(1, 1, 1)
            copy_group(1, 1, 2)
            scale_c(1, 1, 0)
            for b in range(CHUNK_BLOCKS):
                gate_ab(0, b)
            scale_c(1, 1, 1)
            copy_group(1, 1, 3)
            scale_c(1, 1, 2)
            scale_c(1, 1, 3)
            squash(0, 0)
            step(1, 1, True)
            with act.Fori(1, LOOP_PAIRS) as k:
                for par in range(2):
                    step(2 * k + par, par, True)
            step(CHUNKS - 2, 0, True)
            step(CHUNKS - 1, 1, False)
            squash(CHUNKS - 1, 1)

        @block.vector
        def _(dve):
            def scores(g):
                t0, t1 = g * GROUP, (g + 1) * GROUP
                dve.wait_ge(proj_ready, 2 * t1)
                nc.vector.tensor_scalar(s_neg[:, t0:t1], proj[:, t0:t1, FROM_H, S_RIGHT], -1.0, None, ALU.mult)
                nc.vector.tensor_scalar(s_clip[:, t0:t1, :], proj[:, t0:t1, FROM_H, S_LEFT:S_RIGHT + 1],
                                        -EXP_ROOM, EXP_ROOM, ALU.max, ALU.min).then_inc(clip_ready, 1)

            def x_high(t0, t1, done):
                nc.vector.tensor_scalar(x_top[:, t0:t1, :], x_sb[:, t0:t1, :].bitcast(I32),
                                        TOP_12, None, ALU.bitwise_and).then_inc(x_masked, 1)
                dve.wait_ge(x_masked, done)
                nc.vector.tensor_copy(x_parts[:, 0, t0:t1, :], x_top[:, t0:t1, :].bitcast(F32)
                                      ).then_inc(x_hi_ready, 1)

            def w_high(part, c0, c1, done):
                top = w_top[:, 0:KH * (c1 - c0)].rearrange("p (k c) -> p k c", k=KH)
                if done > 1:
                    dve.wait_ge(w_hi_ready, done - 1)
                nc.vector.tensor_scalar(top, w_all[:, part, :, c0:c1].bitcast(I32),
                                        TOP_12, None, ALU.bitwise_and).then_inc(w_masked, 1)
                dve.wait_ge(w_masked, done)
                nc.vector.tensor_copy(w_parts[:, part, 0, :, c0:c1], top.bitcast(F32)).then_inc(w_hi_ready, 1)

            def w_low(part, c0, c1):
                nc.vector.tensor_tensor(w_parts[:, part, 1, :, c0:c1], w_all[:, part, :, c0:c1],
                                        w_parts[:, part, 0, :, c0:c1], ALU.subtract).then_inc(w_lo_ready, 1)

            dve.wait_ge(rows_0_1_loaded, 16)
            x_high(0, 2, 1)
            dve.wait_ge(w_loaded, 16 * 3)
            w_high(FROM_G, 0, MC, 1)
            dve.wait_ge(w_hi_ready, 1)
            w_low(FROM_G, 0, MC)
            dve.wait_ge(w_sa_loaded, 16)
            w_high(FROM_H, 0, d + 2, 2)
            dve.wait_ge(a_loaded, 16)
            for side in (1, 0):
                for k in range(KH):
                    if k or not side:
                        dve.wait_ge(w_vecs_ready, (1 - side) * KH + k)
                    nc.vector.tensor_tensor_reduce(out=a_prod, in0=w_all[:, FROM_H, k, 0:d],
                                                   in1=a_bc[:, side * d:(side + 1) * d], scale=1.0, scalar=0.0,
                                                   op0=ALU.mult, op1=ALU.add,
                                                   accum_out=w_all[:, FROM_H, k, S_LEFT + side:S_LEFT + side + 1]
                                                   ).then_inc(w_vecs_ready, 1)
            dve.wait_ge(w_vecs_ready, 2 * KH)
            w_high(FROM_H, S_LEFT, RC, 3)
            dve.wait_ge(w_hi_ready, 3)
            w_low(FROM_H, S_LEFT, RC)
            dve.wait_ge(x_loaded[0], 16)
            x_high(2, GROUP, 2)
            dve.wait_ge(x_loaded[1], 16)
            x_high(GROUP, 2 * GROUP, 3)
            nc.vector.tensor_reduce(w_max[:, 0:1], w_all[:, :, :, 0:d + 2].rearrange("p s k c -> p (s k) c"),
                                    mybir.AxisListType.XY, ALU.max, apply_absolute_value=True).then_inc(w_max_part, 1)

            steps = [0]

            def settled(op):
                steps[0] += 1
                op.then_inc(cols, 1)
                dve.wait_ge(cols, steps[0])

            for g in range(2, GROUPS):
                dve.wait_ge(x_loaded[g], 16)
                x_high(g * GROUP, (g + 1) * GROUP, g + 2)
            for g in range(SIZED // GROUP, GROUPS):
                op = nc.vector.tensor_reduce(x_size[:, g * GROUP:(g + 1) * GROUP],
                                             x_sb[:, g * GROUP:(g + 1) * GROUP, :], AX_X, ALU.add,
                                             apply_absolute_value=True)
            scores(0)
            dve.wait_ge(w_max_ready, 1)
            dve.wait_ge(x_sizes_ready, SIZED)
            settled(op)
            settled(nc.vector.tensor_scalar(row_bound[:, :], x_size[:, :], w_max[:, 1:2], None, ALU.mult))
            settled(nc.vector.tensor_scalar(row_top[:, :], row_bound[:, :], 1.0, None, ALU.max))
            settled(nc.vector.tensor_scalar(row_inv[:, :].bitcast(I32), row_top[:, :].bitcast(I32),
                                            EXPONENT, EXPONENT, ALU.bitwise_and, ALU.bitwise_xor))
            nc.vector.tensor_scalar(scale[:, 0, :], row_inv[:, :], ROW_SIZE / 2, None,
                                    ALU.mult).then_inc(scale_a_ready, 1)
            nc.vector.tensor_scalar(row_pow[:, :].bitcast(I32), row_top[:, :].bitcast(I32), EXPONENT, None,
                                    ALU.bitwise_and).then_inc(scale_a_ready, 1)

            def scales(g):
                t0, t1 = g * GROUP, (g + 1) * GROUP
                dve.wait_ge(scale_a_ready, 2)
                dve.wait_ge(exps_ready, g + 1)
                settled(nc.vector.reciprocal(p_rec[:, t0:t1], p_top[:, t0:t1]))
                settled(nc.vector.tensor_tensor(p_rest[:, t0:t1], p_raw[:, t0:t1], p_rec[:, t0:t1], ALU.mult))
                nc.vector.tensor_copy(p_top_f[:, t0:t1], p_top[:, t0:t1])
                nc.vector.tensor_tensor(scale[:, 1, t0:t1], q_raw[:, t0:t1], scale[:, 0, t0:t1], ALU.mult)
                nc.vector.tensor_tensor(scale[:, 2, t0:t1], p_rest[:, t0:t1], scale[:, 0, t0:t1],
                                        ALU.mult).then_inc(scale_bc_ready, 1)
                nc.vector.memset(right[:, 1:3, t0:t1, :, d + 1], 0.0)
                dve.wait_ge(scale_bc_ready, g + 1)
                settled(nc.vector.tensor_copy(right[:, 1:3, t0:t1, 0, d], scale[:, 1:3, t0:t1]))
                nc.vector.tensor_tensor(right[:, 1:3, t0:t1, 1, d], scale[:, 1:3, t0:t1],
                                        right[:, 1:3, t0:t1, 0, d], ALU.subtract)

            def low(m, t):
                part, width = (FROM_G, MC) if m == 0 else (FROM_H, d)
                dve.wait_ge(high_ready[m], t + 1)
                nc.vector.scalar_tensor_tensor(out=right[:, m, t, 1, 0:width], in0=proj[:, t, part, 0:width],
                                               scalar=scale[:, m, t:t + 1], in1=right[:, m, t, 0, 0:width],
                                               op0=ALU.mult, op1=ALU.subtract).then_inc(low_ready[m], 1)

            def gate(c, par, g):
                if not (isinstance(c, int) and c < 2) and g == 0:
                    dve.wait_ge(sums_ready, (c - 1) * CHUNK_BLOCKS)
                dve.wait_ge(a_ready, c * GROUPS + g + 1)
                s_row = s_left_row[:, bass.ds(c * CI, CI)]
                for t in range(g * GROUP, (g + 1) * GROUP):
                    op = nc.vector.scalar_tensor_tensor(out=left[:, par, 1, t, :], in0=s_row,
                                                        scalar=s_neg[:, t:t + 1], in1=left[:, par, 0, t, :],
                                                        op0=ALU.is_lt, op1=ALU.mult)
                op.then_inc(b_ready, 1)
                dve.wait_ge(b_ready, c * GROUPS + g + 1)
                ts = slice(g * GROUP, (g + 1) * GROUP)
                nc.vector.tensor_tensor(left[:, par, 2, ts, :], left[:, par, 0, ts, :], left[:, par, 1, ts, :],
                                        ALU.subtract).then_inc(rest_ready, 1)

            def from_a(c, b):
                q = c * CHUNK_BLOCKS + b
                acc_a = acc[b * MATS]
                dve.wait_ge(a_sums_ready, q + 1)
                gate_q = gate_x[:, bass.ds(q, 1), :].rearrange("p q s -> p (q s)")
                nc.vector.scalar_tensor_tensor(out=z[:, b, :], in0=acc_a[:, d:d + 2], scalar=1.0 / ROW_SIZE,
                                               in1=gate_q, op0=ALU.mult, op1=ALU.add)
                nc.vector.scalar_tensor_tensor(out=xb[:, b, :], in0=acc_a[:, 0:d], scalar=1.0 / ROW_SIZE,
                                               in1=b_bc[:, :], op0=ALU.mult, op1=ALU.add).then_inc(z_ready, 1)

            def from_bc(c, b):
                q = c * CHUNK_BLOCKS + b
                acc_b, acc_c = acc[b * MATS + 1], acc[b * MATS + 2]
                dve.wait_ge(sums_ready, q + 1)
                uv_q = uv[:, bass.ds(q, 1), :].rearrange("p q s -> p (q s)")
                nc.vector.tensor_scalar(den_b[:, b, :], acc_b[:, d:d + 1], uv_q[:, 1:2], DEN_EPS,
                                        ALU.mult, ALU.add).then_inc(den_b_ready, 1)
                dve.wait_ge(den_b_ready, q + 1)
                nc.vector.scalar_tensor_tensor(out=den[:, b, :], in0=acc_c[:, d:d + 1], scalar=uv_q[:, 0:1],
                                               in1=den_b[:, b, :], op0=ALU.mult, op1=ALU.add).then_inc(den_ready, 1)
                dve.wait_ge(den_ready, q + 1)
                nc.vector.reciprocal(rden[:, b, :], den[:, b, :]).then_inc(rden_ready, 1)
                dve.wait_ge(rden_ready, q + 1)
                dve.wait_ge(attn_ready, q + 1)
                nc.vector.tensor_scalar(alpha[:, b, :], uv_q, rden[:, b, :], attn[:, b, 0:1], ALU.mult,
                                        ALU.mult).then_inc(alpha_ready, 1)
                dve.wait_ge(alpha_ready, q + 1)
                dve.wait_ge(xb_gated_ready, q + 1)
                nc.vector.scalar_tensor_tensor(out=mix[:, b, :], in0=acc_b[:, 0:d], scalar=alpha[:, b, 1:2],
                                               in1=xb[:, b, :], op0=ALU.mult,
                                               op1=ALU.add).then_inc(mix_b_ready, 1)
                dve.wait_ge(mix_b_ready, q + 1)
                nc.vector.scalar_tensor_tensor(out=mix[:, b, :], in0=acc_c[:, 0:d], scalar=alpha[:, b, 0:1],
                                               in1=mix[:, b, :], op0=ALU.mult, op1=ALU.add).then_inc(sums_read, 1)

            def from_bc_last(c, b):
                q = c * CHUNK_BLOCKS + b
                acc_b, acc_c = acc[b * MATS + 1], acc[b * MATS + 2]
                uv_q = uv[:, q, :]
                dve.wait_ge(last_b_ready, 1)
                nc.vector.tensor_scalar(den_b[:, b, :], acc_b[:, d:d + 1], uv_q[:, 1:2], DEN_EPS,
                                        ALU.mult, ALU.add).then_inc(den_b_ready, 1)
                nc.vector.tensor_scalar(mix[:, b, :], acc_b[:, 0:d], uv_q[:, 1:2], None,
                                        ALU.mult).then_inc(last_mix_b_ready, 1)
                dve.wait_ge(den_b_ready, q + 1)
                dve.wait_ge(last_mix_b_ready, 1)
                dve.wait_ge(attn_ready, q + 1)
                dve.wait_ge(xb_gated_ready, q + 1)
                dve.wait_ge(sums_ready, q + 1)
                nc.vector.scalar_tensor_tensor(out=den[:, b, :], in0=acc_c[:, d:d + 1], scalar=uv_q[:, 0:1],
                                               in1=den_b[:, b, :], op0=ALU.mult, op1=ALU.add).then_inc(den_ready, 1)
                nc.vector.scalar_tensor_tensor(out=mix[:, b, :], in0=acc_c[:, 0:d], scalar=uv_q[:, 0:1],
                                               in1=mix[:, b, :], op0=ALU.mult,
                                               op1=ALU.add).then_inc(last_mix_c_ready, 1)
                dve.wait_ge(den_ready, q + 1)
                nc.vector.reciprocal(rden[:, b, :], den[:, b, :]).then_inc(rden_ready, 1)
                dve.wait_ge(rden_ready, q + 1)
                nc.vector.tensor_scalar(alpha[:, b, 0:1], rden[:, b, :], attn[:, b, 0:1], None,
                                        ALU.mult).then_inc(alpha_ready, 1)
                dve.wait_ge(alpha_ready, q + 1)
                dve.wait_ge(last_mix_c_ready, 1)
                nc.vector.scalar_tensor_tensor(out=mix[:, b, :], in0=mix[:, b, :], scalar=alpha[:, b, 0:1],
                                               in1=xb[:, b, :], op0=ALU.mult, op1=ALU.add).then_inc(sums_read, 1)

            def statistics(c, b):
                q = c * CHUNK_BLOCKS + b
                dve.wait_ge(y_ready, q + 1)
                nc.vector.bn_stats(stats[:, b, :], y[:, b, :]).then_inc(stats_ready, 1)
                if isinstance(c, int) and (c, b) == (CHUNKS - 1, 1):
                    dve.wait_ge(stats_ready, q + 1)
                elif b > 0 or not is_first(c):
                    normalise(c, 0) if b else normalise(c - 1, 1)
                else:
                    dve.wait_ge(stats_ready, q + 1)
                nc.vector.bn_aggr(mean_var[:, b, :], stats[:, b, :]).then_inc(mean_var_ready, 1)
                dve.wait_ge(mean_var_ready, q + 1)
                nc.vector.tensor_scalar(var_eps[:, b, :], mean_var[:, b, 1:2], LN_EPS, None,
                                        ALU.add).then_inc(var_eps_ready, 1)

            def normalise(c, b, more=True):
                q = c * CHUNK_BLOCKS + b
                if more:
                    dve.wait_ge(stats_ready, q + 2)
                dve.wait_ge(rstd_ready, q + 1)
                if not is_first(c):
                    dve.wait_ge(out_stored[b], 16 * c)
                nc.vector.tensor_scalar(y_out[:, b, :], y[:, b, :], mean_var[:, b, 0:1], rstd[:, b, :],
                                        ALU.subtract, ALU.mult).then_inc(out_ready, 1)

            def step(c, par, nxt):
                def gates(g):
                    if nxt:
                        gate(c + 1, 1 - par, g)

                from_bc(c - 1, 1)
                if isinstance(c, int) and c == 1:
                    statistics(0, 0)
                gates(0)
                from_a(c, 0)
                statistics(c - 1, 1)
                gates(1)
                gates(2)
                from_bc(c, 0)
                gates(3)
                from_a(c, 1)
                statistics(c, 0)

            def lows(m, g):
                for t in range(g * GROUP, (g + 1) * GROUP):
                    low(m, t)

            for g in range(GROUPS):
                if g:
                    scores(g)
                if g == 1:
                    dve.wait_ge(s_row_ready, 1)
                    gate(0, 0, 0)
                if g == 2:
                    dve.wait_ge(clip_ready, g + 1)
                    gate(0, 0, g)
                scales(g)
                if g < GROUPS - 1:
                    if g:
                        lows(2, g - 1)
                    if g == 1:
                        gate(0, 0, g)
                    lows(1, g)
                lows(0, g)
            lows(1, GROUPS - 1)
            gate(0, 0, GROUPS - 1)
            for g in (GROUPS - 2, GROUPS - 1):
                lows(2, g)
            dve.wait_ge(u_ready, 1)
            dve.wait_ge(small_loaded, 16 * 3)
            nc.vector.tensor_scalar(uv[:, :, :], u_raw[:, :, :].rearrange("p s t -> p t s"), 1.0 / ROW_SIZE, None,
                                    ALU.mult).then_inc(cols, 1)
            for s in range(2):
                nc.vector.tensor_scalar(gate_x[:, :, s:s + 1], proj[:, :, FROM_H, d + s:d + s + 1],
                                        gate_b[:, s:s + 1], None, ALU.add).then_inc(cols, 1)
            dve.wait_ge(cols, steps[0] + 3)
            dve.wait_ge(s_row_ready, GROUPS)
            from_a(0, 0)
            from_a(0, 1)
            for g in range(GROUPS - 1):
                gate(1, 1, g)
            from_bc(0, 0)
            gate(1, 1, GROUPS - 1)
            step(1, 1, True)
            with dve.Fori(1, LOOP_PAIRS) as k:
                for par in range(2):
                    step(2 * k + par, par, True)
            step(CHUNKS - 2, 0, True)
            step(CHUNKS - 1, 1, False)
            from_bc_last(CHUNKS - 1, 1)
            normalise(CHUNKS - 1, 0, more=False)
            dve.wait_ge(sig_ready, T)
            nc.vector.tensor_tensor(y[:, 1, :], x_sb[:, T - 1, :], mix[:, 1, :], ALU.add).then_inc(y_ready, 1)
            statistics(CHUNKS - 1, 1)
            normalise(CHUNKS - 1, 1, more=False)

        @block.gpsimd
        def _(pool):
            nc.gpsimd.memset(ident_f[:, :], 0.0).then_inc(consts_zeroed, 1)
            nc.gpsimd.memset(ident_b[:, :], 0.0).then_inc(consts_zeroed, 1)
            nc.gpsimd.memset(minus_half[:, :], -0.5)
            pool.wait_ge(consts_zeroed, 2)
            for m in (ident_f, ident_b):
                nc.gpsimd.affine_select(out=m[:, :], in_=m[:, :], compare_op=ALU.not_equal, fill=1.0, base=0,
                                        pattern=[[-1, P]], channel_multiplier=1).then_inc(consts_ready, 1)
            pool.wait_ge(consts_ready, 2)
            nc.gpsimd.tensor_copy(ident_r[:, :], ident_f[:, :]).then_inc(consts_ready, 1)

            def high(m, t):
                nc.gpsimd.tensor_tensor(right[:, m, t, 0, 0:d], proj[:, t, FROM_H, 0:d],
                                        scale[:, m, t:t + 1].to_broadcast([P, d]), ALU.mult).then_inc(high_ready[m], 1)

            def x_low(t):
                if t % GROUP == 0 or t == 2:
                    pool.wait_ge(x_hi_ready, 1 if t == 0 else t // GROUP + 2)
                nc.gpsimd.tensor_tensor(x_parts[:, 1, t, :], x_sb[:, t, :], x_parts[:, 0, t, :],
                                        ALU.subtract).then_inc(x_lo_ready, 1)

            for t in range(2):
                x_low(t)
            pool.wait_ge(w_hi_ready, 2)
            nc.gpsimd.tensor_tensor(w_parts[:, FROM_H, 1, :, 0:d + 2], w_all[:, FROM_H, :, 0:d + 2],
                                    w_parts[:, FROM_H, 0, :, 0:d + 2], ALU.subtract).then_inc(w_lo_h_ready, 1)
            for t in range(2, GROUP):
                x_low(t)
            pool.wait_ge(w_max_part, 1)
            nc.gpsimd.partition_all_reduce(w_max[:, 1:2], w_max[:, 0:1], P, bass.bass_isa.ReduceOp.max
                                           ).then_inc(w_max_ready, 1)

            for t in range(GROUP, 2 * GROUP):
                x_low(t)
            for g in range(GROUPS):
                if g + 2 < GROUPS:
                    for t in range((g + 2) * GROUP, (g + 3) * GROUP):
                        x_low(t)
                pool.wait_ge(scale_bc_ready, g + 1)
                for t in range(g * GROUP, (g + 1) * GROUP):
                    high(1, t)
                if 1 <= g <= FIRST_C:
                    pool.wait_ge(rest_ready, g)
                    for t in range((g - 1) * GROUP, g * GROUP):
                        op = nc.gpsimd.tensor_tensor(left[:, 0, 2, t, :], left[:, 0, 2, t, :],
                                                     p_top[:, t:t + 1].to_broadcast([P, CI]), ALU.mult)
                    op.then_inc(first_c_ready, 1)
                for t in range(g * GROUP, (g + 1) * GROUP):
                    high(2, t)
            def finish(c, b, recycled, residual=True):
                q = c * CHUNK_BLOCKS + b
                if residual:
                    pool.wait_ge(sig_ready, q + 1)
                if recycled and residual:
                    pool.wait_ge(out_ready, q - 1)
                if residual:
                    nc.gpsimd.tensor_tensor(y[:, b, :], x_sb[:, bass.ds(q, 1), :].rearrange("p q d -> p (q d)"),
                                            mix[:, b, :], ALU.add).then_inc(y_ready, 1)
                pool.wait_ge(var_eps_ready, q + 1)
                nc.gpsimd.tensor_tensor(rstd[:, b, :], var_eps[:, b, :], minus_half[:, :],
                                        ALU.pow).then_inc(rstd_ready, 1)

            for b in range(CHUNK_BLOCKS):
                finish(0, b, False)
            with pool.Fori(1, CHUNKS - 1) as c:
                for b in range(CHUNK_BLOCKS):
                    finish(c, b, True)
            finish(CHUNKS - 1, 0, True)
            finish(CHUNKS - 1, 1, True, residual=False)


_INS = ["x", "adj", "L0_gnn_W_sa", "L0_gnn_a_sa", "L0_gnn_W_gcnb", "L0_gnn_b_gcnb",
        "L0_gnn_Wa", "L0_gnn_ba", "L0_gnn_Wb", "L0_gnn_bb"]


def kernel(**inputs):
    import numpy as _np
    import concourse.bacc as _bacc
    from concourse import mybir as _mybir
    from concourse.bass_utils import run_bass_kernel_spmd as _run

    nc = _bacc.Bacc("TRN2", target_bir_lowering=False, num_devices=1)
    arrays, args = {}, []
    for name in _INS:
        a = _np.ascontiguousarray(inputs[name])
        arrays[f"in_{name}_dram"] = a
        args.append(nc.dram_tensor(f"in_{name}_dram", a.shape, _mybir.dt.from_np(a.dtype), kind="ExternalInput").ap())
    o = nc.dram_tensor("out_dram", tuple(inputs["x"].shape), _mybir.dt.float32, kind="ExternalOutput").ap()
    build(nc, *args, o)
    r = _run(nc, [arrays], core_ids=[0])
    return r.results[0]["out_dram"]
```
